# Optimizing a Trainium2 kernel written in Bass

```python
import numpy as np
import jax
import jax.numpy as jnp

def _softmax(x, axis=-1):
    return jax.nn.softmax(x, axis=axis)

def _gelu(x):
    return jax.nn.gelu(x, approximate=True)

def _silu(x):
    return jax.nn.silu(x)

def _sigmoid(x):
    return jax.nn.sigmoid(x)

def _layernorm(x, axis=-1, eps=1e-05):
    m = jnp.mean(x, axis=axis, keepdims=True)
    v = jnp.var(x, axis=axis, keepdims=True)
    return (x - m) / jnp.sqrt(v + eps)

def _scatter_add(tgt, idx, src, axis=0):
    return tgt.at[idx].add(src)

def _segment_sum(src, seg, n):
    return jax.ops.segment_sum(src, seg, n)
kernel_name = 'mk_vit_tower_d1_tok_img1024_r4_39790a'

def setup_inputs(seed: int=0):
    np.random.seed(seed)
    _w = jnp.asarray

    def _rec_inputs():
        import jax
        import jax.numpy as jnp
        _rk = jax.random.key(seed)
        x = -0.00016672 + 0.999947 * jax.random.normal(jax.random.fold_in(_rk, 1), (16, 3, 96, 96), jnp.float32)
        return x
    x = _rec_inputs()

    def _L0_tok_setup():
        import jax, jax.numpy as jnp
        import numpy as np
        IMG = 96
        PATCH = 16
        C_IN = 3
        EMBED = 256
        NPH = IMG // PATCH
        NUM_PATCHES = NPH * NPH
        PATCH_DIM = PATCH * PATCH * C_IN
        key = jax.random.key(seed)
        k_x, k_w, k_b, k_cls, k_pos = jax.random.split(key, 5)
        x = jax.random.normal(k_x, (64, C_IN, IMG, IMG), dtype=jnp.float32)
        W = jax.random.normal(k_w, (EMBED, PATCH_DIM), dtype=jnp.float32) * (1.0 / np.sqrt(PATCH_DIM))
        b = jax.random.normal(k_b, (EMBED,), dtype=jnp.float32) * 0.01
        cls_token = jax.random.normal(k_cls, (1, 1, EMBED), dtype=jnp.float32) * 0.02
        pos_embed = jax.random.normal(k_pos, (1, NUM_PATCHES + 1, EMBED), dtype=jnp.float32) * 0.02
        return {'x': x, 'W': W, 'b': b, 'cls_token': cls_token, 'pos_embed': pos_embed}
    _L0_tok_all = _L0_tok_setup()
    _L0_tok_in = {k: v for k, v in _L0_tok_all.items() if k in ('W', 'b', 'cls_token', 'pos_embed')}
    del _L0_tok_all

    def _L0_attn_setup():
        import jax, jax.numpy as jnp
        import numpy as np
        DIM = 256
        NUM_HEADS = 16
        HEAD_DIM = DIM // NUM_HEADS
        EPS = 1e-06

        def layer_norm(x, gamma, beta):
            mu = jnp.mean(x, axis=-1, keepdims=True)
            var = jnp.mean(jnp.square(x - mu), axis=-1, keepdims=True)
            return (x - mu) / jnp.sqrt(var + EPS) * gamma + beta

        def apply_rope(q, k):
            seq_len, head_dim = (q.shape[1], q.shape[3])
            half = head_dim // 2
            freq_range = jnp.arange(half, dtype=jnp.float32) / half
            inv_freq = 1.0 / 10000.0 ** freq_range
            t = jnp.arange(seq_len, dtype=jnp.float32)
            freqs = jnp.outer(t, inv_freq)
            emb = jnp.concatenate([freqs, freqs], axis=-1)
            cos = jnp.cos(emb)[None, :, None, :]
            sin = jnp.sin(emb)[None, :, None, :]

            def rotate_half(x):
                x1, x2 = (x[..., :half], x[..., half:])
                return jnp.concatenate([-x2, x1], axis=-1)
            return (q * cos + rotate_half(q) * sin, k * cos + rotate_half(k) * sin)
        key = jax.random.key(seed)
        ks = jax.random.split(key, 4)
        B, S = (2, 512)
        x = jax.random.normal(ks[0], (B, S, DIM), dtype=jnp.float32)
        lim_qkv = float(np.sqrt(6.0 / (DIM + 3 * DIM)))
        w_qkv = jax.random.uniform(ks[1], (3 * DIM, DIM), dtype=jnp.float32, minval=-lim_qkv, maxval=lim_qkv)
        lim_p = float(np.sqrt(6.0 / (DIM + DIM)))
        w_proj = jax.random.uniform(ks[2], (DIM, DIM), dtype=jnp.float32, minval=-lim_p, maxval=lim_p)
        b_proj = jnp.zeros((DIM,), dtype=jnp.float32)
        q_gamma = jnp.ones((HEAD_DIM,), dtype=jnp.float32)
        q_beta = jnp.zeros((HEAD_DIM,), dtype=jnp.float32)
        k_gamma = jnp.ones((HEAD_DIM,), dtype=jnp.float32)
        k_beta = jnp.zeros((HEAD_DIM,), dtype=jnp.float32)
        return {'x': x, 'w_qkv': w_qkv, 'w_proj': w_proj, 'b_proj': b_proj, 'q_gamma': q_gamma, 'q_beta': q_beta, 'k_gamma': k_gamma, 'k_beta': k_beta}
    _L0_attn_all = _L0_attn_setup()
    _L0_attn_in = {k: v for k, v in _L0_attn_all.items() if k in ('w_qkv', 'w_proj', 'b_proj', 'q_gamma', 'q_beta', 'k_gamma', 'k_beta')}
    del _L0_attn_all

    def _L0_ffn_setup():
        import jax, jax.numpy as jnp
        import numpy as np
        DIM = 256
        HIDDEN = 768
        SCALE = 1.0 / 127.0

        def _dequant(w_int, dtype):
            return w_int.astype(dtype) * jnp.asarray(SCALE, dtype)
        key = jax.random.key(seed)
        k_x, k_g, k_u, k_d = jax.random.split(key, 4)
        x = jax.random.normal(k_x, (4, 512, DIM), dtype=jnp.float32)
        w_gate = jax.random.randint(k_g, (HIDDEN, DIM), -127, 128, dtype=jnp.int32)
        w_up = jax.random.randint(k_u, (HIDDEN, DIM), -127, 128, dtype=jnp.int32)
        w_down = jax.random.randint(k_d, (DIM, HIDDEN), -127, 128, dtype=jnp.int32)
        return {'x': x, 'w_gate': w_gate, 'w_up': w_up, 'w_down': w_down}
    _L0_ffn_all = _L0_ffn_setup()
    _L0_ffn_in = {k: v for k, v in _L0_ffn_all.items() if k in ('w_gate', 'w_up', 'w_down')}
    del _L0_ffn_all
    return {'x': x, 'L0_tok_W': _L0_tok_in['W'], 'L0_tok_b': _L0_tok_in['b'], 'L0_tok_cls_token': _L0_tok_in['cls_token'], 'L0_tok_pos_embed': _L0_tok_in['pos_embed'], 'L0_attn_w_qkv': _L0_attn_in['w_qkv'], 'L0_attn_w_proj': _L0_attn_in['w_proj'], 'L0_attn_b_proj': _L0_attn_in['b_proj'], 'L0_attn_q_gamma': _L0_attn_in['q_gamma'], 'L0_attn_q_beta': _L0_attn_in['q_beta'], 'L0_attn_k_gamma': _L0_attn_in['k_gamma'], 'L0_attn_k_beta': _L0_attn_in['k_beta'], 'L0_ffn_w_gate': _L0_ffn_in['w_gate'], 'L0_ffn_w_up': _L0_ffn_in['w_up'], 'L0_ffn_w_down': _L0_ffn_in['w_down']}

def reference(x, L0_tok_W, L0_tok_b, L0_tok_cls_token, L0_tok_pos_embed, L0_attn_w_qkv, L0_attn_w_proj, L0_attn_b_proj, L0_attn_q_gamma, L0_attn_q_beta, L0_attn_k_gamma, L0_attn_k_beta, L0_ffn_w_gate, L0_ffn_w_up, L0_ffn_w_down):
    import jax
    import jax.numpy as jnp

    def _L0_tok_ref(x, W, b, cls_token, pos_embed):
        import jax, jax.numpy as jnp
        import numpy as np
        IMG = 96
        PATCH = 16
        C_IN = 3
        EMBED = 256
        NPH = IMG // PATCH
        NUM_PATCHES = NPH * NPH
        PATCH_DIM = PATCH * PATCH * C_IN
        B, C, H, Wd = x.shape
        nph, npw = (H // PATCH, Wd // PATCH)
        patches = x.reshape(B, C, nph, PATCH, npw, PATCH)
        patches = patches.transpose(0, 2, 4, 1, 3, 5)
        patches = patches.reshape(B, nph * npw, C * PATCH * PATCH)
        proj = jnp.einsum('bnd,ed->bne', patches, W) + b
        cls = jnp.broadcast_to(cls_token, (B, 1, cls_token.shape[-1]))
        out = jnp.concatenate([cls, proj], axis=1) + pos_embed
        return out

    def _L0_attn_ref(x, w_qkv, w_proj, b_proj, q_gamma, q_beta, k_gamma, k_beta):
        import jax, jax.numpy as jnp
        import numpy as np
        DIM = 256
        NUM_HEADS = 16
        HEAD_DIM = DIM // NUM_HEADS
        EPS = 1e-06

        def layer_norm(x, gamma, beta):
            mu = jnp.mean(x, axis=-1, keepdims=True)
            var = jnp.mean(jnp.square(x - mu), axis=-1, keepdims=True)
            return (x - mu) / jnp.sqrt(var + EPS) * gamma + beta

        def apply_rope(q, k):
            seq_len, head_dim = (q.shape[1], q.shape[3])
            half = head_dim // 2
            freq_range = jnp.arange(half, dtype=jnp.float32) / half
            inv_freq = 1.0 / 10000.0 ** freq_range
            t = jnp.arange(seq_len, dtype=jnp.float32)
            freqs = jnp.outer(t, inv_freq)
            emb = jnp.concatenate([freqs, freqs], axis=-1)
            cos = jnp.cos(emb)[None, :, None, :]
            sin = jnp.sin(emb)[None, :, None, :]

            def rotate_half(x):
                x1, x2 = (x[..., :half], x[..., half:])
                return jnp.concatenate([-x2, x1], axis=-1)
            return (q * cos + rotate_half(q) * sin, k * cos + rotate_half(k) * sin)
        B, S, C = x.shape
        H, D = (NUM_HEADS, HEAD_DIM)
        qkv = jnp.einsum('bsc,oc->bso', x, w_qkv).reshape(B, S, 3, H, D)
        q = layer_norm(qkv[:, :, 0], q_gamma, q_beta)
        k = layer_norm(qkv[:, :, 1], k_gamma, k_beta)
        v = qkv[:, :, 2]
        q, k = apply_rope(q, k)
        scale = D ** (-0.5)
        q = q.astype(jnp.float32) * scale
        k = k.astype(jnp.float32)
        v = v.astype(jnp.float32)
        attn = jnp.einsum('bqhd,bkhd->bhqk', q, k)
        attn = jax.nn.softmax(attn, axis=-1)
        out = jnp.einsum('bhqk,bkhd->bqhd', attn, v).reshape(B, S, C)
        out = jnp.einsum('bsc,oc->bso', out, w_proj) + b_proj
        return out

    def _L0_ffn_ref(x, w_gate, w_up, w_down):
        import jax, jax.numpy as jnp
        import numpy as np
        DIM = 256
        HIDDEN = 768
        SCALE = 1.0 / 127.0

        def _dequant(w_int, dtype):
            return w_int.astype(dtype) * jnp.asarray(SCALE, dtype)
        wg = _dequant(w_gate, x.dtype)
        wu = _dequant(w_up, x.dtype)
        wd = _dequant(w_down, x.dtype)
        gate = jnp.einsum('bsd,hd->bsh', x, wg)
        up = jnp.einsum('bsd,hd->bsh', x, wu)
        h = jax.nn.silu(gate) * up
        return jnp.einsum('bsh,dh->bsd', h, wd)
    h = _L0_tok_ref(x, L0_tok_W, L0_tok_b, L0_tok_cls_token, L0_tok_pos_embed)
    h = h + _L0_attn_ref(_layernorm(h, axis=-1), L0_attn_w_qkv, L0_attn_w_proj, L0_attn_b_proj, L0_attn_q_gamma, L0_attn_q_beta, L0_attn_k_gamma, L0_attn_k_beta)
    h = h + _L0_ffn_ref(_layernorm(h, axis=-1), L0_ffn_w_gate, L0_ffn_w_up, L0_ffn_w_down)
    return h

_drawn_inputs = setup_inputs


def setup_inputs(seed=0):
    import zlib

    import numpy as np

    out = dict(_drawn_inputs(seed))
    spreads = {'L0_attn_b_proj': (0.0, 0.1),
     'L0_attn_q_gamma': (1.0, 0.2),
     'L0_attn_q_beta': (0.0, 0.1),
     'L0_attn_k_gamma': (1.0, 0.2),
     'L0_attn_k_beta': (0.0, 0.337)}
    factors = {'L0_tok_b': 3.088}
    for name, (base, spread) in spreads.items():
        noise = np.random.default_rng([zlib.crc32(name.encode()), seed]).standard_normal(out[name].shape)
        drawn = base * np.exp(spread * noise) if base else spread * noise
        out[name] = jnp.asarray(drawn.astype(out[name].dtype))
    for name, factor in factors.items():
        out[name] = (out[name] * factor).astype(out[name].dtype)
    return out
```

```python
from contextlib import ExitStack

import numpy as np

import concourse.bass as bass
from concourse import mybir

IMAGES, CHANNELS, SIDE, PATCH = 16, 3, 96, 16
GRID = SIDE // PATCH
TOK = GRID * GRID + 1
T = IMAGES * TOK
P = 128
DIM, HEADS, HD, HIDDEN = 256, 16, 16, 768
HALF = HD // 2
PATCH_DIM = CHANNELS * PATCH * PATCH
KP = PATCH_DIM // P
KD = DIM // P
KH = HIDDEN // P
TILES = [(a, min(P, T - a)) for a in range(0, T, P)]
NT = len(TILES)
PAIRS = IMAGES // 2
COLS = T // 2
EPS, EPS_HEAD = 1e-5, 1e-6
CODE_SCALE = 1.0 / 127.0

SLOT_HEAD = [8 * c + 2 * i + e for i in range(4) for c in range(2) for e in range(2)]
REP = 3
GROUPS = 6
GROUP_SLOT = [0, 3, 6, 9, 12, 13]
VALUE_SLOTS = [[3 * g + r for g in range(5)] + ([15] if r == 2 else []) for r in range(REP)]
HV = HD + 1
QPAD = T + 64 - TOK
ROWS = 64 + TOK


def build(nc, xT, wT, selT, tok_rows, wqkT, wvT, wpT, b_proj, gammas, betas, tab, tabT, maskT,
          wgT, wuT, wdT, out):
    f32, f32r = mybir.dt.float32, mybir.dt.float32r
    ALU, ACT, AX = mybir.AluOpType, mybir.ActivationFunctionType, mybir.AxisListType

    with ExitStack() as ctx:
        def sb(name, shape, dt=f32):
            return ctx.enter_context(nc.sbuf_tensor(name, shape, dt))

        def sem(name):
            return ctx.enter_context(nc.semaphore(name))

        x_in = sb("x_in", [P, KP, T])
        x_hi, x_lo = sb("x_hi", [P, KP, T], f32r), sb("x_lo", [P, KP, T], f32r)
        hid_hi, hid_lo = x_hi, x_lo
        w_in = sb("w_in", [P, KP, DIM])
        w_hi, w_lo = sb("w_hi", [P, KP, DIM], f32r), sb("w_lo", [P, KP, DIM], f32r)
        sel_in, sel = sb("sel_in", [TOK + 2, T]), sb("sel", [TOK + 2, T], f32r)
        rows_in = sb("rows_in", [TOK + 2, DIM])
        rows_hi, rows_lo = sb("rows_hi", [TOK + 2, DIM], f32r), sb("rows_lo", [TOK + 2, DIM], f32r)
        wqk_in = sb("wqk_in", [P, KD, 2 * DIM])
        wqk_mean = sb("wqk_mean", [P, KD, 2 * HEADS])
        wqk_hi, wqk_lo = sb("wqk_hi", [P, KD, 2 * DIM], f32r), sb("wqk_lo", [P, KD, 2 * DIM], f32r)
        wv_in = sb("wv_in", [P, KD, DIM])
        wv_hi, wv_lo = sb("wv_hi", [P, KD, DIM], f32r), sb("wv_lo", [P, KD, DIM], f32r)
        wp_in = sb("wp_in", [P, KD, DIM])
        wp_hi, wp_lo = sb("wp_hi", [P, KD, DIM], f32r), sb("wp_lo", [P, KD, DIM], f32r)
        bp_in = sb("bp_in", [1, DIM])
        bp_hi, bp_lo = sb("bp_hi", [1, DIM], f32r), sb("bp_lo", [1, DIM], f32r)
        one_row_in, one_row = sb("one_row_in", [1, P]), sb("one_row", [1, P], f32r)
        wg, wu = sb("wg", [P, KD, HIDDEN], f32r), sb("wu", [P, KD, HIDDEN], f32r)
        wd = sb("wd", [P, KH, DIM], f32r)
        gam = sb("gam", [P, 2, 2, HD])
        bet = sb("bet", [P, 2, 2])
        tab_sb = sb("tab_sb", [P, 2, NT, 2, HD])
        rope_a, rope_b = sb("rope_a", [P, NT, 2, HD]), sb("rope_b", [P, NT, 2, HD])
        tabT_sb = sb("tabT_sb", [P, 2, 2, TOK])
        bT = sb("bT", [P, 2, 2, TOK])
        betaT = sb("betaT", [P, 2, TOK])
        kbeta = sb("kbeta", [P, 2, TOK])
        qbeta_all = sb("qbeta_all", [P, IMAGES, TOK])
        kbeta_all = sb("kbeta_all", [P, 2, IMAGES, TOK])
        mask = sb("mask", [P, 2])
        ident = sb("ident", [P, P])
        eps_ln, eps_head = sb("eps_ln", [P, 1]), sb("eps_head", [P, 1])
        h0 = sb("h0", [P, NT, DIM])
        x1 = sb("x1", [P, NT, DIM])
        stats, mv = sb("stats", [P, 2, NT, 6]), sb("mv", [P, 2, NT, 2])
        std, rstd, shift = sb("std", [P, 2, NT]), sb("rstd", [P, 2, NT]), sb("shift", [P, 2, NT])
        ln = sb("ln", [P, 2, DIM])
        lnT_hi, lnT_lo = sb("lnT_hi", [P, KD, T], f32r), sb("lnT_lo", [P, KD, T], f32r)
        square = sb("square", [P, 2, 2 * DIM])
        part_a, part_b = sb("part_a", [P, 2, 2 * DIM]), sb("part_b", [P, 2, 2 * DIM])
        qk = sb("qk", [P, 2, 2 * DIM])
        ssum, hstd, hrstd = sb("ssum", [P, NT, 32]), sb("hstd", [P, NT, 32]), sb("hrstd", [P, NT, 32])
        qT = sb("qT", [P, KD, QPAD])
        kT = sb("kT", [P, KD, 2, T])
        v_tok = sb("v_tok", [P, NT, REP, GROUPS, HV])
        v_rep = sb("v_rep", [P, IMAGES, REP, GROUPS, HV])
        top = sb("top", [P, 2, HEADS])
        x_room = x_in[:].rearrange("p k n -> p (k n)")
        w_room = [w[:].rearrange("p k n -> p (k n)") for w in (w_in, w_hi, w_lo)]
        logit = x_room[:, 0:T].rearrange("p (h k) -> p h k", k=TOK)
        prob = x_room[:, T:3 * T].rearrange("p (u n) -> p u n", u=2)
        probT = x_room[:, 3 * T:3 * T + 2 * GROUPS * ROWS].rearrange("p (u g n) -> p u g n", u=2, g=GROUPS)
        rsum = sb("rsum", [P, 2, HEADS])
        attn = sb("attn", [P, 2, HEADS, HD])
        attnT_hi, attnT_lo = (w[:, 0:KD * T].rearrange("p (c n) -> p c n", c=KD) for w in w_room[1:])
        silu = w_room[0][:, 0:2 * COLS].rearrange("p (u n) -> p u n", u=2)
        hid = w_room[0][:, 2 * COLS:4 * COLS].rearrange("p (u n) -> p u n", u=2)
        res = h0

        ps = ctx.enter_context(nc.psum_tensor("ps", [P, 8, 512], f32))

        patch_in = [sem(f"patch_in{k}") for k in range(KP)]
        rows_loaded, wqk_loaded = sem("rows_loaded"), sem("wqk_loaded")
        wv_loaded, wp_loaded, tab_loaded = sem("wv_loaded"), sem("wp_loaded"), sem("tab_loaded")
        ffn_loaded = [sem(f"ffn_loaded{k}") for k in range(3)]
        ident_made, padded, ones_made = sem("ident_made"), sem("padded"), sem("ones_made")
        sel_hi_made, rows_lo_made = sem("sel_hi_made"), sem("rows_lo_made")
        patch_hi, patch_lo = sem("patch_hi"), sem("patch_lo")
        wqk_meaned, wqk_centred, wqk_hi_made, wqk_split = map(
            sem, ["wqk_meaned", "wqk_centred", "wqk_hi_made", "wqk_split"])
        wv_split, wp_split = sem("wv_split"), sem("wp_split")
        rope_made, tabs_step, beta_made = sem("rope_made"), sem("tabs_step"), sem("beta_made")
        embedded, h0_kept, stat_step, std_made, shift_made = map(
            sem, ["embedded", "h0_kept", "stat_step", "std_made", "shift_made"])
        normed, lnT_in, lnT_hi_made, lnT_split = map(
            sem, ["normed", "lnT_in", "lnT_hi_made", "lnT_split"])
        qk_in, squared, summed, hstd_made, hrstd_made = map(
            sem, ["qk_in", "squared", "summed", "hstd_made", "hrstd_made"])
        parts_made, parts_added, roped = map(sem, ["parts_made", "parts_added", "roped"])
        qkT_in, q_ready, k_ready = sem("qkT_in"), sem("q_ready"), sem("k_ready")
        v_in, v_kept = sem("v_in"), sem("v_kept")
        v_spread = [sem(f"v_spread{p}") for p in range(PAIRS)]
        scored, topped, shifted, prob_made = map(sem, ["scored", "topped", "shifted", "prob_made"])
        probT_in, probT_kept, mixed, rsum_made, attn_made = map(
            sem, ["probT_in", "probT_kept", "mixed", "rsum_made", "attn_made"])
        attnT_in, attnT_hi_made, attnT_split = map(sem, ["attnT_in", "attnT_hi_made", "attnT_split"])
        projected, x1_made = sem("projected"), sem("x1_made")
        gate_in, up_in, silu_made, hid_made, hid_hi_made, hid_split = map(
            sem, ["gate_in", "up_in", "silu_made", "hid_made", "hid_hi_made", "hid_split"])
        down_in, res_made, stored = sem("down_in"), sem("res_made"), sem("stored")

        LN_BANK, QKT_BANK = 5, 7
        QK_BANK, V_BANK = [6, 1, 2, 3, 4], 0
        PT_BANK, MIX_BANK, ATT_BANK = 4, 6, 7
        GATE_BANK, UP_BANK = [6, 7], [0, 1]
        DOWN_BANK = [2, 3, 4, 2, 3]

        def images_after(t):
            return (TILES[t][0] + TILES[t][1]) // TOK

        def tile_for(tokens):
            return -(-tokens // P)

        def spreads(p):
            for b in (2 * p, 2 * p + 1):
                for t in range(b * TOK // P, tile_for((b + 1) * TOK)):
                    lo, hi = max(b * TOK, t * P), min((b + 1) * TOK, t * P + P)
                    for r in range(REP):
                        yield b, t, r, lo, hi

        block = ctx.enter_context(nc.Block())

        @block.sync
        def _(sp):
            for k in range(KP):
                sp.dma_start(x_in[:, k, :], xT[:, k, :]).then_inc(patch_in[k], 16)
                if k == 0:
                    sp.dma_start(rows_in[:], tok_rows).then_inc(rows_loaded, 16)
                    sp.dma_start(sel_in[:], selT).then_inc(rows_loaded, 16)
            sp.dma_start(wqk_in[:], wqkT).then_inc(wqk_loaded, 16)
            sp.dma_start(tab_sb[:], tab).then_inc(tab_loaded, 16)
            sp.dma_start(gam[:], gammas).then_inc(tab_loaded, 16)
            sp.dma_start(bet[:], betas).then_inc(tab_loaded, 16)
            sp.dma_start(tabT_sb[:], tabT).then_inc(tab_loaded, 16)
            sp.dma_start(mask[:], maskT).then_inc(tab_loaded, 16)
            sp.dma_start(wv_in[:], wvT).then_inc(wv_loaded, 16)
            sp.dma_start(wp_in[:], wpT).then_inc(wp_loaded, 16)
            sp.dma_start(bp_in[:], b_proj).then_inc(wp_loaded, 16)
            sp.wait_ge(ones_made, 4)
            for p in range(PAIRS):
                sp.wait_ge(v_kept, 2 * tile_for(2 * (p + 1) * TOK))
                for b, t, r, lo, hi in spreads(p):
                    k = r * TOK + lo - b * TOK
                    sp.dma_start(v_rep[k:k + hi - lo, b, r, :, :],
                                 v_tok[lo - t * P:hi - t * P, t, r, :, :]).then_inc(v_spread[p], 16)
            for t, (a, n) in enumerate(TILES):
                sp.wait_ge(res_made, t + 1)
                sp.dma_start(out[a:a + n, :], res[0:n, t, :]).then_inc(stored, 16)
            sp.wait_ge(stored, 16 * NT)

        @block.gpsimd
        def _(pool):
            nc.gpsimd.memset(ident[:], 0.0).then_inc(ident_made, 1)
            pool.wait_ge(ident_made, 1)
            nc.gpsimd.affine_select(out=ident[:], in_=ident[:], compare_op=ALU.not_equal, fill=1.0,
                                    base=0, pattern=[[-1, P]], channel_multiplier=1).then_inc(ident_made, 1)
            nc.gpsimd.memset(eps_ln[:], EPS).then_inc(padded, 1)
            nc.gpsimd.memset(eps_head[:], EPS_HEAD).then_inc(padded, 1)
            nc.gpsimd.memset(one_row_in[:], 1.0).then_inc(padded, 1)
            nc.gpsimd.memset(qT[:, :, T:QPAD], 0.0).then_inc(padded, 1)
            pool.dma_start(wg[:], wgT).then_inc(ffn_loaded[0], 16)
            pool.dma_start(wu[:], wuT).then_inc(ffn_loaded[1], 16)
            pool.dma_start(wd[:], wdT).then_inc(ffn_loaded[2], 16)
            nc.gpsimd.memset(v_rep[:, 0:8], 0.0).then_inc(ones_made, 1)
            nc.gpsimd.memset(v_rep[:, 8:16], 0.0).then_inc(ones_made, 1)
            nc.gpsimd.memset(v_tok[:, :, :, :, 0:HD], 0.0).then_inc(ones_made, 1)
            nc.gpsimd.memset(v_tok[:, :, :, :, HD:HV], 1.0).then_inc(ones_made, 1)
            pool.wait_ge(tab_loaded, 80)
            nc.gpsimd.tensor_tensor(out=rope_a[:], in0=tab_sb[:, 0],
                                    in1=gam[:, None, 0].broadcast_to([P, NT, 2, HD]),
                                    op=ALU.mult).then_inc(rope_made, 1)
            nc.gpsimd.tensor_tensor(out=rope_b[:], in0=tab_sb[:, 1],
                                    in1=gam[:, None, 1].broadcast_to([P, NT, 2, HD]),
                                    op=ALU.mult).then_inc(rope_made, 1)
            for j in range(2):
                for w in range(2):
                    nc.gpsimd.tensor_scalar(bT[:, j, w, :], tabT_sb[:, j, w, :], bet[:, j, w:w + 1],
                                            None, ALU.mult).then_inc(tabs_step, 1)
            pool.wait_ge(tabs_step, 4)
            nc.gpsimd.tensor_tensor(out=betaT[:], in0=bT[:, 0], in1=bT[:, 1],
                                    op=ALU.add).then_inc(tabs_step, 1)
            pool.wait_ge(tabs_step, 5)
            for e in range(2):
                nc.gpsimd.tensor_scalar(kbeta[:, e, :], betaT[:, 1, :], mask[:, e:e + 1], None,
                                        ALU.mult).then_inc(tabs_step, 1)
            nc.gpsimd.tensor_copy(qbeta_all[:], betaT[:, 0:1, :].broadcast_to([P, IMAGES, TOK])
                                  ).then_inc(beta_made, 1)
            pool.wait_ge(tabs_step, 7)
            for e in range(2):
                nc.gpsimd.tensor_copy(kbeta_all[:, e], kbeta[:, e:e + 1, :].broadcast_to([P, IMAGES, TOK])
                                      ).then_inc(beta_made, 1)

            def rope_tile(t):
                n = TILES[t][1]
                pool.wait_ge(parts_made, 3 * (t + 1))
                nc.gpsimd.tensor_tensor(out=part_a[0:n, t % 2, :], in0=part_a[0:n, t % 2, :],
                                        in1=part_b[0:n, t % 2, :], op=ALU.add).then_inc(parts_added, 1)
                pool.wait_ge(parts_added, t + 1)
                pool.wait_ge(hrstd_made, t + 1)
                if t >= 2:
                    pool.wait_ge(qkT_in, t - 1)
                nc.gpsimd.tensor_tensor(
                    out=qk[0:n, t % 2, :].rearrange("p (h d) -> p h d", d=HD),
                    in0=part_a[0:n, t % 2, :].rearrange("p (h d) -> p h d", d=HD),
                    in1=hrstd[0:n, t, :, None].broadcast_to([n, 2 * HEADS, HD]),
                    op=ALU.mult).then_inc(roped, 1)

            def split(hi, lo, src, semaphore, n0):
                nc.gpsimd.tensor_copy(hi, src).then_inc(semaphore, 1)
                pool.wait_ge(semaphore, n0 + 1)
                nc.gpsimd.tensor_tensor(out=lo, in0=src, in1=hi.bitcast(f32),
                                        op=ALU.subtract).then_inc(semaphore, 1)

            pool.wait_ge(wv_loaded, 16)
            split(wv_hi[:], wv_lo[:], wv_in[:], wv_split, 0)
            for t in range(NT):
                rope_tile(t)
            pool.wait_ge(wp_loaded, 32)
            split(wp_hi[:], wp_lo[:], wp_in[:], wp_split, 0)
            split(bp_hi[:], bp_lo[:], bp_in[:], wp_split, 2)

        @block.scalar
        def _(act):
            for k in range(KP):
                act.dma_start(w_in[:, k, :], wT[:, k, :]).then_inc(patch_in[k], 16)
            act.wait_ge(padded, 4)
            nc.scalar.copy(one_row[:], one_row_in[:]).then_inc(sel_hi_made, 1)
            for k in range(KP):
                act.wait_ge(patch_in[k], 32)
                nc.scalar.copy(x_hi[:, k, :], x_in[:, k, :]).then_inc(patch_hi, 1)
                nc.scalar.copy(w_hi[:, k, :], w_in[:, k, :]).then_inc(patch_hi, 1)
                if k == 0:
                    act.wait_ge(rows_loaded, 32)
                    nc.scalar.copy(rows_hi[:], rows_in[:]).then_inc(sel_hi_made, 1)
                    nc.scalar.copy(sel[:], sel_in[:]).then_inc(sel_hi_made, 1)
            act.wait_ge(wqk_centred, 1)
            nc.scalar.copy(wqk_hi[:], wqk_in[:]).then_inc(wqk_hi_made, 1)

            def deviation(which, t):
                n, i = TILES[t][1], which * NT + t
                act.wait_ge(stat_step, 2 * (i + 1))
                nc.scalar.activation(std[0:n, which, t:t + 1], mv[0:n, which, t, 1:2], ACT.Sqrt,
                                     bias=eps_ln[0:n, 0:1]).then_inc(std_made, 1)

            def apply_norm(which, t, src):
                n, i = TILES[t][1], which * NT + t
                act.wait_ge(shift_made, 2 * (i + 1))
                if i >= 2:
                    act.wait_ge(lnT_in, i - 1)
                nc.scalar.activation(ln[0:n, i % 2, :], src, ACT.Identity,
                                     bias=shift[0:n, which, t:t + 1],
                                     scale=rstd[0:n, which, t:t + 1]).then_inc(normed, 1)

            def lnT_upper(which, t):
                a, n = TILES[t]
                i = which * NT + t
                act.wait_ge(lnT_in, i + 1)
                nc.scalar.copy(lnT_hi[:, :, a:a + n],
                               ps[:, LN_BANK, 0:KD * n].rearrange("p (c n) -> p c n", c=KD)
                               ).then_inc(lnT_hi_made, 1)

            def heads_and_values(t):
                n = TILES[t][1]
                act.wait_ge(qk_in, t + 1)
                if t >= 2:
                    act.wait_ge(summed, t - 1)
                nc.scalar.activation(square[0:n, t % 2, :], ps[0:n, QK_BANK[t], :], ACT.Square
                                     ).then_inc(squared, 1)
                act.wait_ge(v_in, t + 1)
                if t == 0:
                    act.wait_ge(ones_made, 4)
                for r0, r1, g, c0, c1 in ((0, 2, 5, 0, 160), (2, 3, 6, 160, 256)):
                    nc.scalar.copy(v_tok[0:n, t, r0:r1, 0:g, 0:HD],
                                   ps[0:n, V_BANK, c0:c1].rearrange("p (r g d) -> p r g d", g=g, d=HD)
                                   ).then_inc(v_kept, 1)
                act.wait_ge(summed, t + 1)
                nc.scalar.activation(hstd[0:n, t, :], ssum[0:n, t, :], ACT.Sqrt, scale=1.0 / HD,
                                     bias=eps_head[0:n, 0:1]).then_inc(hstd_made, 1)

            act.wait_ge(embedded, 1)
            for t in range(NT):
                n = TILES[t][1]
                deviation(0, t)
                nc.scalar.copy(h0[0:n, t, :], ps[0:n, t, 0:DIM]).then_inc(h0_kept, 1)
                apply_norm(0, t, ps[0:n, t, 0:DIM])
                lnT_upper(0, t)
                if t >= 1:
                    heads_and_values(t - 1)
            heads_and_values(NT - 1)

            def attnT_upper(p):
                act.wait_ge(attnT_in, p + 1)
                for j in range(2):
                    nc.scalar.copy(attnT_hi[:, :, (2 * p + j) * TOK:(2 * p + j + 1) * TOK],
                                   ps[:, ATT_BANK, 0:KD * ROWS].rearrange("p (c n) -> p c n", c=KD)
                                   [:, :, 64 * j:64 * j + TOK]).then_inc(attnT_hi_made, 1)

            for p in range(PAIRS):
                act.wait_ge(shifted, p + 1)
                if p >= 2:
                    act.wait_ge(probT_in, 2 * (p - 1))
                nc.scalar.activation(prob[:, p % 2, :], logit[:].rearrange("p h k -> p (h k)"), ACT.Exp
                                     ).then_inc(prob_made, 1)
                if p >= 2:
                    attnT_upper(p - 2)
                act.wait_ge(probT_in, 2 * p + 1)
                if p >= 2:
                    act.wait_ge(mixed, p - 1)
                nc.scalar.copy(probT[0:REP * TOK, p % 2, 0:3, :],
                               ps[0:REP * TOK, PT_BANK, 0:3 * ROWS].rearrange("p (g n) -> p g n", g=3)
                               ).then_inc(probT_kept, 1)
            attnT_upper(PAIRS - 2)
            attnT_upper(PAIRS - 1)

            for t in range(NT):
                n = TILES[t][1]
                deviation(1, t)
                apply_norm(1, t, x1[0:n, t, :])
                lnT_upper(1, t)

            def hidden_upper(u):
                half, j = divmod(u, KH)
                act.wait_ge(hid_made, u + 1)
                nc.scalar.copy(hid_hi[:, j, half * COLS:(half + 1) * COLS], hid[:, u % 2, :]
                               ).then_inc(hid_hi_made, 1)

            for u in range(2 * KH):
                act.wait_ge(gate_in, u + 1)
                if u >= 2:
                    act.wait_ge(hid_made, u - 1)
                nc.scalar.activation(silu[:, u % 2, :], ps[:, GATE_BANK[u % 2], 0:COLS], ACT.Silu,
                                     scale=CODE_SCALE).then_inc(silu_made, 1)
                if u >= 1:
                    hidden_upper(u - 1)
            hidden_upper(2 * KH - 1)

        @block.vector
        def _(dve):
            for k in range(KP):
                dve.wait_ge(patch_hi, 2 * k + 1)
                nc.vector.tensor_tensor(out=x_lo[:, k, :], in0=x_in[:, k, :],
                                        in1=x_hi[:, k, :].bitcast(f32), op=ALU.subtract
                                        ).then_inc(patch_lo, 1)
                dve.wait_ge(patch_hi, 2 * k + 2)
                nc.vector.tensor_tensor(out=w_lo[:, k, :], in0=w_in[:, k, :],
                                        in1=w_hi[:, k, :].bitcast(f32), op=ALU.subtract
                                        ).then_inc(patch_lo, 1)
            dve.wait_ge(sel_hi_made, 3)
            nc.vector.tensor_tensor(out=rows_lo[:], in0=rows_in[:], in1=rows_hi[:].bitcast(f32),
                                    op=ALU.subtract).then_inc(rows_lo_made, 1)
            dve.wait_ge(wqk_loaded, 16)
            wqk_heads = wqk_in[:].rearrange("p c (h d) -> p (c h) d", d=HD)
            means = wqk_mean[:].rearrange("p c h -> p (c h)")
            nc.vector.tensor_reduce(means, wqk_heads, AX.X, ALU.add).then_inc(wqk_meaned, 1)
            dve.wait_ge(wqk_meaned, 1)
            nc.vector.tensor_scalar(means, means, 1.0 / HD, None, ALU.mult).then_inc(wqk_meaned, 1)
            dve.wait_ge(wqk_meaned, 2)
            nc.vector.tensor_tensor(out=wqk_heads, in0=wqk_heads,
                                    in1=means[:, :, None].broadcast_to([P, KD * 2 * HEADS, HD]),
                                    op=ALU.subtract).then_inc(wqk_centred, 1)
            dve.wait_ge(wqk_hi_made, 1)
            nc.vector.tensor_tensor(out=wqk_lo[:], in0=wqk_in[:], in1=wqk_hi[:].bitcast(f32),
                                    op=ALU.subtract).then_inc(wqk_split, 1)

            def statistics(which, t, src):
                n, i = TILES[t][1], which * NT + t
                nc.vector.bn_stats(stats[0:n, which, t, :], src).then_inc(stat_step, 1)
                dve.wait_ge(stat_step, 2 * i + 1)
                nc.vector.bn_aggr(mv[0:n, which, t, :], stats[0:n, which, t, :]).then_inc(stat_step, 1)

            def shift_of(which, t):
                n, i = TILES[t][1], which * NT + t
                dve.wait_ge(std_made, i + 1)
                nc.vector.reciprocal(rstd[0:n, which, t:t + 1], std[0:n, which, t:t + 1]
                                     ).then_inc(shift_made, 1)
                dve.wait_ge(shift_made, 2 * i + 1)
                nc.vector.tensor_scalar(shift[0:n, which, t:t + 1], mv[0:n, which, t, 0:1],
                                        rstd[0:n, which, t:t + 1], -1.0, ALU.mult, ALU.mult
                                        ).then_inc(shift_made, 1)

            def lnT_lower(which, t):
                a, n = TILES[t]
                dve.wait_ge(lnT_hi_made, which * NT + t + 1)
                nc.vector.tensor_tensor(out=lnT_lo[:, :, a:a + n],
                                        in0=ps[:, LN_BANK, 0:KD * n].rearrange("p (c n) -> p c n", c=KD),
                                        in1=lnT_hi[:, :, a:a + n].bitcast(f32), op=ALU.subtract
                                        ).then_inc(lnT_split, 1)

            def rope_parts(t):
                n = TILES[t][1]
                dve.wait_ge(squared, t + 1)
                if t == 0:
                    dve.wait_ge(rope_made, 2)
                if t >= 2:
                    dve.wait_ge(roped, t - 1)
                x = ps[0:n, QK_BANK[t], :].rearrange("p (w h d) -> p w h d", w=2, d=HD)
                a = part_a[0:n, t % 2, :].rearrange("p (w h d) -> p w h d", w=2, d=HD)
                b = part_b[0:n, t % 2, :].rearrange("p (w h d) -> p w h d", w=2, d=HD)
                nc.vector.tensor_reduce(ssum[0:n, t, :],
                                        square[0:n, t % 2, :].rearrange("p (h d) -> p h d", d=HD),
                                        AX.X, ALU.add).then_inc(summed, 1)
                nc.vector.tensor_tensor(out=a, in0=x,
                                        in1=rope_a[0:n, t, :, None].broadcast_to([n, 2, HEADS, HD]),
                                        op=ALU.mult).then_inc(parts_made, 1)
                for s in range(2):
                    o, i = slice(s * HALF, (s + 1) * HALF), slice((1 - s) * HALF, (2 - s) * HALF)
                    nc.vector.tensor_tensor(out=b[:, :, :, o], in0=x[:, :, :, i],
                                            in1=rope_b[0:n, t, :, None, o].broadcast_to([n, 2, HEADS, HALF]),
                                            op=ALU.mult).then_inc(parts_made, 1)
                dve.wait_ge(hstd_made, t + 1)
                nc.vector.reciprocal(hrstd[0:n, t, :], hstd[0:n, t, :]).then_inc(hrstd_made, 1)

            def keep_qkT(t):
                a, n = TILES[t]
                dve.wait_ge(qkT_in, t + 1)
                if t == 0:
                    dve.wait_ge(beta_made, 3)
                src = ps[:, QKT_BANK, 0:4 * n].rearrange("p (w c n) -> p w c n", w=2, c=KD)
                qb = qbeta_all[:].rearrange("p b k -> p (b k)")
                kb = kbeta_all[:].rearrange("p e b k -> p e (b k)")
                nc.vector.tensor_tensor(out=qT[:, :, a:a + n], in0=src[:, 0],
                                        in1=qb[:, None, a:a + n].broadcast_to([P, KD, n]),
                                        op=ALU.add).then_inc(q_ready, 1)
                for e in range(2):
                    nc.vector.scalar_tensor_tensor(out=kT[:, :, e, a:a + n], in0=src[:, 1],
                                                   scalar=mask[:, e:e + 1],
                                                   in1=kb[:, e:e + 1, a:a + n].broadcast_to([P, KD, n]),
                                                   op0=ALU.mult, op1=ALU.add).then_inc(k_ready, 1)

            for t in range(NT):
                n = TILES[t][1]
                if t == 0:
                    dve.wait_ge(embedded, 1)
                statistics(0, t, ps[0:n, t, 0:DIM])
                shift_of(0, t)
                lnT_lower(0, t)
                if t >= 1:
                    rope_parts(t - 1)
                if t >= 2:
                    keep_qkT(t - 2)
            rope_parts(NT - 1)
            keep_qkT(NT - 2)
            keep_qkT(NT - 1)

            def normalise(p):
                dve.wait_ge(mixed, p + 1)
                o = ps[0:ROWS, MIX_BANK, 0:HEADS * HV].rearrange("p (h d) -> p h d", d=HV)
                nc.vector.reciprocal(rsum[0:ROWS, p % 2, :], o[:, :, HD]).then_inc(rsum_made, 1)
                dve.wait_ge(rsum_made, p + 1)
                if p >= 2:
                    dve.wait_ge(attnT_in, p - 1)
                nc.vector.tensor_tensor(out=attn[0:ROWS, p % 2], in0=o[:, :, 0:HD],
                                        in1=rsum[0:ROWS, p % 2, :, None].broadcast_to([ROWS, HEADS, HD]),
                                        op=ALU.mult).then_inc(attn_made, 1)

            def attnT_lower(p):
                dve.wait_ge(attnT_hi_made, 2 * p + 2)
                for j in range(2):
                    cols = slice((2 * p + j) * TOK, (2 * p + j + 1) * TOK)
                    nc.vector.tensor_tensor(
                        out=attnT_lo[:, :, cols],
                        in0=ps[:, ATT_BANK, 0:KD * ROWS].rearrange("p (c n) -> p c n", c=KD)
                        [:, :, 64 * j:64 * j + TOK],
                        in1=attnT_hi[:, :, cols].bitcast(f32), op=ALU.subtract).then_inc(attnT_split, 1)

            for p in range(PAIRS):
                dve.wait_ge(scored, p + 1)
                s = ps[:, 0:4, 0:4 * TOK].rearrange("p i (g k) -> p i g k", k=TOK)
                top4 = top[:, p % 2, :].rearrange("p (i g) -> p i g", i=4)
                nc.vector.tensor_reduce(top4, s, AX.X, ALU.max).then_inc(topped, 1)
                dve.wait_ge(topped, p + 1)
                if p >= 1:
                    dve.wait_ge(prob_made, p)
                nc.vector.tensor_tensor(out=logit[:].rearrange("p (i g) k -> p i g k", i=4), in0=s,
                                        in1=top4[:, :, :, None].broadcast_to([P, 4, 4, TOK]),
                                        op=ALU.subtract).then_inc(shifted, 1)
                if p >= 1:
                    normalise(p - 1)
                if p >= 2:
                    attnT_lower(p - 2)
                dve.wait_ge(probT_in, 2 * p + 2)
                if p >= 2:
                    dve.wait_ge(mixed, p - 1)
                nc.vector.tensor_copy(probT[0:REP * TOK, p % 2, 3:6, :],
                                      ps[0:REP * TOK, PT_BANK + 1, 0:3 * ROWS].rearrange("p (g n) -> p g n", g=3)
                                      ).then_inc(probT_kept, 1)
            attnT_lower(PAIRS - 2)
            normalise(PAIRS - 1)
            attnT_lower(PAIRS - 1)

            for t in range(NT):
                n = TILES[t][1]
                dve.wait_ge(projected, t + 1)
                if t == 0:
                    dve.wait_ge(h0_kept, NT)
                nc.vector.tensor_tensor(out=x1[0:n, t, :], in0=ps[0:n, t, 0:DIM], in1=h0[0:n, t, :],
                                        op=ALU.add).then_inc(x1_made, 1)
                dve.wait_ge(x1_made, t + 1)
                statistics(1, t, x1[0:n, t, :])
                shift_of(1, t)
                lnT_lower(1, t)

            def hidden_lower(u):
                half, j = divmod(u, KH)
                cols = slice(half * COLS, (half + 1) * COLS)
                dve.wait_ge(hid_hi_made, u + 1)
                nc.vector.tensor_tensor(out=hid_lo[:, j, cols], in0=hid[:, u % 2, :],
                                        in1=hid_hi[:, j, cols].bitcast(f32), op=ALU.subtract
                                        ).then_inc(hid_split, 1)

            def result(t):
                n = TILES[t][1]
                dve.wait_ge(down_in, t + 1)
                nc.vector.scalar_tensor_tensor(out=res[0:n, t, :], in0=ps[0:n, DOWN_BANK[t], 0:DIM],
                                               scalar=CODE_SCALE, in1=x1[0:n, t, :],
                                               op0=ALU.mult, op1=ALU.add).then_inc(res_made, 1)

            for u in range(2 * KH):
                dve.wait_ge(silu_made, u + 1)
                dve.wait_ge(up_in, u + 1)
                if u >= 2:
                    dve.wait_ge(hid_split, u - 1)
                nc.vector.scalar_tensor_tensor(out=hid[:, u % 2, :], in0=ps[:, UP_BANK[u % 2], 0:COLS],
                                               scalar=CODE_SCALE, in1=silu[:, u % 2, :],
                                               op0=ALU.mult, op1=ALU.mult).then_inc(hid_made, 1)
                if u >= 1:
                    hidden_lower(u - 1)
                if u >= KH + 2 and u < KH + 4:
                    result(u - KH - 2)
            hidden_lower(2 * KH - 1)
            for t in range(2, NT):
                result(t)

        @block.tensor
        def _(pe):
            def split_product(dst, steps, first=True, last=True):
                for i, (lhs, rhs) in enumerate(steps):
                    m = nc.tensor.matmul(dst, lhs, rhs, start=first and i == 0,
                                         stop=last and i == len(steps) - 1)
                return m

            for k in range(KP):
                pe.wait_ge(patch_hi, 2 * k + 2)
                pe.wait_ge(patch_lo, 2 * k + 2)
                for t, (a, n) in enumerate(TILES):
                    split_product(ps[0:n, t, 0:DIM],
                                  [(x_hi[:, k, a:a + n], w_hi[:, k, :]), (x_hi[:, k, a:a + n], w_lo[:, k, :]),
                                   (x_lo[:, k, a:a + n], w_hi[:, k, :])], k == 0, False)
            pe.wait_ge(rows_lo_made, 1)
            for t, (a, n) in enumerate(TILES):
                split_product(ps[0:n, t, 0:DIM], [(sel[:, a:a + n], rows_hi[:]), (sel[:, a:a + n], rows_lo[:])],
                              False, True).then_inc(embedded, 1)

            def transpose_ln(which, t):
                n, i = TILES[t][1], which * NT + t
                pe.wait_ge(normed, i + 1)
                if i == 0:
                    pe.wait_ge(ident_made, 2)
                if i >= 1:
                    pe.wait_ge(lnT_split, i)
                for c in range(KD):
                    m = nc.tensor.transpose(ps[:, LN_BANK, c * n:(c + 1) * n],
                                            ln[0:n, i % 2, c * P:(c + 1) * P], ident[0:n, 0:n])
                m.then_inc(lnT_in, 1)

            def project_qkv(t):
                a, n = TILES[t]
                pe.wait_ge(lnT_split, t + 1)
                if t == 0:
                    pe.wait_ge(wqk_split, 1)
                    pe.wait_ge(wv_split, 2)
                pe.wait_ge(normed, t + 1)
                pe.wait_ge(h0_kept, t + 1)
                both = [(w, c) for w in range(3) for c in range(KD)]
                lhs = [lnT_hi, lnT_hi, lnT_lo]
                split_product(ps[0:n, QK_BANK[t], :],
                              [(lhs[w][:, c, a:a + n], [wqk_hi, wqk_lo, wqk_hi][w][:, c, :]) for w, c in both]
                              ).then_inc(qk_in, 1)
                if t >= 1:
                    pe.wait_ge(v_kept, 2 * t)
                split_product(ps[0:n, V_BANK, 0:DIM],
                              [(lhs[w][:, c, a:a + n], [wv_hi, wv_lo, wv_hi][w][:, c, :]) for w, c in both]
                              ).then_inc(v_in, 1)

            def transpose_qk(t):
                n = TILES[t][1]
                pe.wait_ge(roped, t + 1)
                if t >= 1:
                    pe.wait_ge(k_ready, 2 * t)
                for w in range(4):
                    m = nc.tensor.transpose(ps[:, QKT_BANK, w * n:(w + 1) * n],
                                            qk[0:n, t % 2, w * P:(w + 1) * P], ident[0:n, 0:n])
                m.then_inc(qkT_in, 1)

            for t in range(NT):
                transpose_ln(0, t)
                project_qkv(t)
                if t >= 1:
                    transpose_qk(t - 1)
            transpose_qk(NT - 1)

            def score(p):
                pe.wait_ge(k_ready, 2 * min(NT, tile_for(2 * p * TOK + TOK + 64)))
                if p == 0:
                    pe.wait_ge(padded, 4)
                    pe.wait_ge(parts_made, 3 * NT)
                    pe.wait_ge(v_kept, 2 * NT)
                if p >= 1:
                    pe.wait_ge(shifted, p)
                for j in range(2):
                    b = 2 * p + j
                    for c in range(KD):
                        for i in range(4):
                            rows = slice(32 * i, 32 * i + 32)
                            m = nc.tensor.matmul(ps[64 * j:64 * j + 64, i, 2 * c * TOK:2 * (c + 1) * TOK],
                                                 qT[rows, c, b * TOK:b * TOK + 64],
                                                 kT[rows, c, :, b * TOK:(b + 1) * TOK], start=True, stop=True)
                m.then_inc(scored, 1)

            def mix(p):
                pe.wait_ge(probT_kept, 2 * (p + 1))
                pe.wait_ge(v_spread[p], 16 * len(list(spreads(p))))
                if p >= 1:
                    pe.wait_ge(attn_made, p)
                for j in range(2):
                    q = slice(64 * j, 64 if j == 0 else ROWS)
                    for g in range(GROUPS):
                        if g < GROUPS - 1:
                            cols = slice(g * REP * HV, (g + 1) * REP * HV)
                            v = v_rep[0:REP * TOK, 2 * p + j, :, g, :]
                        else:
                            cols = slice(15 * HV, 16 * HV)
                            v = v_rep[0:REP * TOK, 2 * p + j, REP - 1, g, :]
                        m = nc.tensor.matmul(ps[q, MIX_BANK, cols], probT[0:REP * TOK, p % 2, g, q], v,
                                             start=True, stop=True)
                m.then_inc(mixed, 1)

            def transpose_attn(p):
                pe.wait_ge(attn_made, p + 1)
                if p >= 1:
                    pe.wait_ge(attnT_split, 2 * p)
                flat = attn[0:ROWS, p % 2].rearrange("p h d -> p (h d)")
                for c in range(KD):
                    m = nc.tensor.transpose(ps[:, ATT_BANK, c * ROWS:(c + 1) * ROWS],
                                            flat[:, c * P:(c + 1) * P], ident[0:ROWS, 0:ROWS])
                m.then_inc(attnT_in, 1)

            def transpose_prob(p):
                pe.wait_ge(prob_made, p + 1)
                for g in range(GROUPS):
                    if p >= 1 and g % 3 == 0:
                        pe.wait_ge(probT_kept, 2 * p)
                    a = GROUP_SLOT[g] * TOK
                    m = nc.tensor.transpose(ps[0:REP * TOK, PT_BANK + g // 3, (g % 3) * ROWS:(g % 3 + 1) * ROWS],
                                            prob[0:ROWS, p % 2, a:a + REP * TOK], ident[0:ROWS, 0:ROWS])
                    if g % 3 == 2:
                        m.then_inc(probT_in, 1)

            for p in range(PAIRS):
                score(p)
                if p >= 1:
                    mix(p - 1)
                if p >= 2:
                    transpose_attn(p - 2)
                if p == 0:
                    pe.wait_ge(lnT_split, NT)
                transpose_prob(p)
            transpose_attn(PAIRS - 2)
            mix(PAIRS - 1)
            transpose_attn(PAIRS - 1)

            pe.wait_ge(wp_split, 4)
            pe.wait_ge(sel_hi_made, 1)
            pe.wait_ge(shifted, PAIRS)

            def project_out(t):
                a, n = TILES[t]
                pe.wait_ge(attnT_split, 2 * min(PAIRS, -(-(a + n) // (2 * TOK))))
                steps = [(one_row[:, 0:n], bp_hi[:]), (one_row[:, 0:n], bp_lo[:])]
                for c in range(KD):
                    steps += [(attnT_hi[:, c, a:a + n], wp_hi[:, c, :]), (attnT_hi[:, c, a:a + n], wp_lo[:, c, :]),
                              (attnT_lo[:, c, a:a + n], wp_hi[:, c, :])]
                split_product(ps[0:n, t, 0:DIM], steps).then_inc(projected, 1)

            for t in range(NT):
                project_out(t)
                if t >= 1:
                    transpose_ln(1, t - 1)
            transpose_ln(1, NT - 1)

            for k in range(3):
                pe.wait_ge(ffn_loaded[k], 16)

            def gate_up(u):
                half, j = divmod(u, KH)
                pe.wait_ge(lnT_split, NT + tile_for((half + 1) * COLS))
                cols, units = slice(half * COLS, (half + 1) * COLS), slice(j * P, (j + 1) * P)
                if u >= 2:
                    pe.wait_ge(silu_made, u - 1)
                else:
                    pe.wait_ge(x1_made, NT)
                split_product(ps[:, GATE_BANK[u % 2], 0:COLS],
                              [(wg[:, c, units], x[:, c, cols]) for c in range(KD) for x in (lnT_hi, lnT_lo)]
                              ).then_inc(gate_in, 1)
                if u >= 2:
                    pe.wait_ge(hid_made, u - 1)
                split_product(ps[:, UP_BANK[u % 2], 0:COLS],
                              [(wu[:, c, units], x[:, c, cols]) for c in range(KD) for x in (lnT_hi, lnT_lo)]
                              ).then_inc(up_in, 1)

            def down(t):
                a, n = TILES[t]
                pe.wait_ge(hid_split, KH * (1 if a + n <= COLS else 2))
                if t >= 3:
                    pe.wait_ge(res_made, t - 2)
                split_product(ps[0:n, DOWN_BANK[t], 0:DIM],
                              [(h[:, j, a:a + n], wd[:, j, :]) for j in range(KH) for h in (hid_hi, hid_lo)]
                              ).then_inc(down_in, 1)

            for u in range(2 * KH):
                gate_up(u)
                if u >= KH + 1 and u < KH + 3:
                    down(u - KH - 1)
            for t in range(2, NT):
                down(t)


def _chunks(a):
    k = a.shape[0] // P
    return np.ascontiguousarray(a.reshape(k, P, -1).transpose(1, 0, 2))


def _rotary():
    inv = (1.0 / np.float32(10000.0) ** (np.arange(HALF, dtype=np.float32) / np.float32(HALF))).astype(np.float32)
    freq = np.outer(np.arange(TOK, dtype=np.float32), inv).astype(np.float32)
    cos = np.cos(np.concatenate([freq, freq], -1))
    sin = np.sin(np.concatenate([-freq, freq], -1))
    scale = np.float32(HD ** -0.5)
    return np.stack([np.stack([cos * scale, cos]), np.stack([sin * scale, sin])]).astype(np.float32)


def kernel(x, L0_tok_W, L0_tok_b, L0_tok_cls_token, L0_tok_pos_embed, L0_attn_w_qkv, L0_attn_w_proj,
           L0_attn_b_proj, L0_attn_q_gamma, L0_attn_q_beta, L0_attn_k_gamma, L0_attn_k_beta,
           L0_ffn_w_gate, L0_ffn_w_up, L0_ffn_w_down):
    import concourse.bacc as bacc
    from concourse.bass_utils import run_bass_kernel_spmd

    x = np.asarray(x)
    f = np.float32
    patches = x.reshape(IMAGES, CHANNELS, GRID, PATCH, GRID, PATCH).transpose(1, 3, 5, 0, 2, 4)
    cols = np.zeros((PATCH_DIM, IMAGES, TOK), f)
    cols[:, :, 1:] = patches.reshape(PATCH_DIM, IMAGES, TOK - 1)
    sel = np.zeros((TOK + 2, IMAGES, TOK), f)
    for k in range(TOK):
        sel[k, :, k] = 1
    sel[TOK, :, 1:] = 1
    sel[TOK + 1, :, 0] = 1
    tok_rows = np.concatenate([np.asarray(L0_tok_pos_embed).reshape(TOK, DIM), np.asarray(L0_tok_b).reshape(1, DIM),
                               np.asarray(L0_tok_cls_token).reshape(1, DIM)])
    w_qkv, w_proj = np.asarray(L0_attn_w_qkv), np.asarray(L0_attn_w_proj)
    heads = np.arange(DIM).reshape(HEADS, HD)
    v_rows = np.concatenate([heads[SLOT_HEAD[s]] for slots in VALUE_SLOTS for s in slots])
    p_rows = np.concatenate([heads[h] for h in SLOT_HEAD])
    rot = _rotary()
    pos = np.arange(NT * P) % TOK
    tab = rot[:, :, pos, :].reshape(2, 2, NT, P, HD).transpose(3, 0, 2, 1, 4)
    tabT = np.tile(rot.transpose(3, 0, 1, 2), (P // HD, 1, 1, 1))
    swap = np.r_[HALF:HD, 0:HALF]
    g = [np.asarray(L0_attn_q_gamma), np.asarray(L0_attn_k_gamma)]
    b = [np.asarray(L0_attn_q_beta), np.asarray(L0_attn_k_beta)]
    gammas = np.broadcast_to(np.stack([np.stack(g), np.stack([v[swap] for v in g])]), (P, 2, 2, HD))
    betas = np.tile(np.stack([np.stack(b, -1), np.stack([v[swap] for v in b], -1)], 1), (P // HD, 1, 1))
    odd = (np.arange(P) // HD % 2).astype(f)

    arrays = {
        "xT": _chunks(cols.reshape(PATCH_DIM, T)),
        "wT": _chunks(np.asarray(L0_tok_W).T),
        "selT": sel.reshape(TOK + 2, T),
        "tok_rows": tok_rows,
        "wqkT": _chunks(w_qkv[:2 * DIM].T),
        "wvT": _chunks(w_qkv[2 * DIM:][v_rows].T),
        "wpT": _chunks(w_proj.T[p_rows]),
        "b_proj": np.asarray(L0_attn_b_proj).reshape(1, DIM),
        "gammas": gammas,
        "betas": betas,
        "tab": tab,
        "tabT": tabT,
        "maskT": np.stack([1 - odd, odd], -1),
        "wgT": _chunks(np.asarray(L0_ffn_w_gate).T),
        "wuT": _chunks(np.asarray(L0_ffn_w_up).T),
        "wdT": _chunks(np.asarray(L0_ffn_w_down).T),
    }
    nc = bacc.Bacc("TRN2", target_bir_lowering=False, num_devices=1)
    given, args = {}, {}
    for name, a in arrays.items():
        a = np.ascontiguousarray(a)
        given[f"in_{name}"] = a
        args[name] = nc.dram_tensor(f"in_{name}", a.shape, mybir.dt.from_np(a.dtype), kind="ExternalInput").ap()
    out = nc.dram_tensor("out", (T, DIM), mybir.dt.float32, kind="ExternalOutput").ap()
    build(nc, out=out, **args)
    r = run_bass_kernel_spmd(nc, [given], core_ids=[0])
    return r.results[0]["out"].reshape(IMAGES, TOK, DIM)
```

```python
from contextlib import ExitStack

import numpy as np

import concourse.bass as bass
from concourse import mybir

IMAGES, CHANNELS, SIDE, PATCH = 16, 3, 96, 16
GRID = SIDE // PATCH
TOK = GRID * GRID + 1
T = IMAGES * TOK
P = 128
DIM, HEADS, HD, HIDDEN = 256, 16, 16, 768
HALF = HD // 2
PATCH_DIM = CHANNELS * PATCH * PATCH
KP = PATCH_DIM // P
KD = DIM // P
KH = HIDDEN // P
TILES = [(a, min(P, T - a)) for a in range(0, T, P)]
NT = len(TILES)
PAIRS = IMAGES // 2
COLS = T // 2
EPS, EPS_HEAD = 1e-5, 1e-6
CODE_SCALE = 1.0 / 127.0

CH = P // HD
REP = 3
GROUPS = 6
GROUP_HEAD = [0, 3, 6, 9, 12, 13]
VALUE_HEADS = [[3 * g + r for g in range(5)] + ([15] if r == 2 else []) for r in range(REP)]
HV = HD + 2
WIDE = [64, TOK + 1]
ROWS = 64 + WIDE[1]
V_RING, K_RING = 3, 3

BEFORE = [("embed", 0), ("embed", 1), ("scale", 0), ("norm1", 0), ("embed", 2), ("scale", 1), ("qkv", 0),
          ("norm1", 1), ("embed", 3), ("scale", 2), ("rms", 0), ("qkv", 1), ("norm1", 2), ("embed", 4),
          ("rope", 0), ("scale", 3), ("rms", 1), ("norm1", 3), ("scale", 4), ("rope", 1)]
BESIDE = [[("qkv", 2), ("norm1", 4), ("rms", 2)],
          [("rope", 2), ("qkv", 3), ("rms", 3)],
          [("rope", 3), ("qkv", 4), ("rms", 4)],
          [("rope", 4)],
          [("proj", 0), ("scale2", 0)],
          [("proj", 1), ("norm2", 0), ("scale2", 1)],
          [("norm2", 1)],
          [("proj", 2), ("scale2", 2)]]
AFTER = [("proj", 3), ("norm2", 2), ("scale2", 3), ("proj", 4), ("norm2", 3), ("scale2", 4), ("norm2", 4)]
CUTS = [("add", 0), ("add", 1), ("cut", 0), ("cut", 1), ("cut", 2), ("add", 2), ("add", 3), ("cut", 3),
        ("cut", 4), ("add", 4), ("cut", 5), ("wp", 0), ("cut", 6), ("cut", 7)]
EARLY = 3


def build(nc, xT, wT, selT, tok_rows, wqkT, wvT, wpT, b_proj, gammas, betas, tab, tabT, maskT,
          wgT, wuT, wdT, out):
    f32, f32r = mybir.dt.float32, mybir.dt.float32r
    ALU, ACT, AX = mybir.AluOpType, mybir.ActivationFunctionType, mybir.AxisListType

    with ExitStack() as ctx:
        def sb(name, shape, dt=f32):
            return ctx.enter_context(nc.sbuf_tensor(name, shape, dt))

        def sem(name):
            return ctx.enter_context(nc.semaphore(name))

        x_in = sb("x_in", [P, KP, T])
        x_hi, x_lo = sb("x_hi", [P, KP, T], f32r), sb("x_lo", [P, KP, T], f32r)
        hid_hi, hid_lo = x_hi, x_lo
        w_in = sb("w_in", [P, KP, DIM])
        w_hi, w_lo = sb("w_hi", [P, KP, DIM], f32r), sb("w_lo", [P, KP, DIM], f32r)
        sel_in, sel = sb("sel_in", [TOK + 2, T]), sb("sel", [TOK + 2, T], f32r)
        rows_in = sb("rows_in", [TOK + 2, DIM])
        rows_hi, rows_lo = sb("rows_hi", [TOK + 2, DIM], f32r), sb("rows_lo", [TOK + 2, DIM], f32r)
        wqk_in = sb("wqk_in", [P, KD, 2 * DIM])
        wqk_mean = sb("wqk_mean", [P, KD, 2 * HEADS])
        wqk_hi, wqk_lo = sb("wqk_hi", [P, KD, 2 * DIM], f32r), sb("wqk_lo", [P, KD, 2 * DIM], f32r)
        wv_in = sb("wv_in", [P, KD, DIM])
        wv_hi, wv_lo = sb("wv_hi", [P, KD, DIM], f32r), sb("wv_lo", [P, KD, DIM], f32r)
        wp_in = sb("wp_in", [P, KD, DIM])
        wp_hi, wp_lo = sb("wp_hi", [P, KD, DIM], f32r), sb("wp_lo", [P, KD, DIM], f32r)
        bp_in = sb("bp_in", [1, DIM])
        bp_hi, bp_lo = sb("bp_hi", [1, DIM], f32r), sb("bp_lo", [1, DIM], f32r)
        one_row_in, one_row = sb("one_row_in", [1, P]), sb("one_row", [1, P], f32r)
        wg, wu = sb("wg", [P, KD, HIDDEN], f32r), sb("wu", [P, KD, HIDDEN], f32r)
        wd = sb("wd", [P, KH, DIM], f32r)
        gam = sb("gam", [P, 2, 2, HD])
        bet = sb("bet", [P, 2, 2])
        tab_sb = sb("tab_sb", [P, 2, NT, 2, HD])
        rope_a, rope_b = sb("rope_a", [P, NT, 2, HD]), sb("rope_b", [P, NT, 2, HD])
        tabT_sb = sb("tabT_sb", [P, 2, 2, TOK])
        bT = sb("bT", [P, 2, 2, TOK])
        betaT = sb("betaT", [P, 2, TOK])
        beta_all = sb("beta_all", [P, 2, IMAGES, TOK])
        mask = sb("mask", [P, CH])
        ident = sb("ident", [P, P])
        h0 = sb("h0", [P, NT, DIM])
        x1 = sb("x1", [P, NT, DIM])
        stats, mv = sb("stats", [P, 2, NT, 6]), sb("mv", [P, 2, NT, 2])
        var, log_var, guess, newton, rstd, shift = (
            sb(name, [P, 2 * NT]) for name in ("var", "log_var", "guess", "newton", "rstd", "shift"))
        lnT_hi, lnT_lo = sb("lnT_hi", [P, KD, T], f32r), sb("lnT_lo", [P, KD, T], f32r)
        square = sb("square", [P, 2, 2 * DIM])
        part_a, part_b = sb("part_a", [P, 2, 2 * DIM]), sb("part_b", [P, 2, 2 * DIM])
        qk = sb("qk", [P, 2, 2 * DIM])
        ssum, hlog, hguess = sb("ssum", [P, NT, 32]), sb("hlog", [P, NT, 32]), sb("hguess", [P, NT, 32])
        hvar, hnewton, hrstd = sb("hvar", [P, NT, 32]), sb("hnewton", [P, NT, 32]), sb("hrstd", [P, NT, 32])
        qT, kT = sb("qT", [P, KD, T + 1]), sb("kT", [P, KD, T])
        k_heads = sb("k_heads", [P, K_RING, KD, CH, 2 * TOK])
        v_tok = sb("v_tok", [P, NT, REP, GROUPS, HV])
        v_rep = sb("v_rep", [P, V_RING, 2, REP, GROUPS, HV])
        top = sb("top", [P, 2, HEADS])
        x_room = x_in[:].rearrange("p k n -> p (k n)")
        w_room = [w[:].rearrange("p k n -> p (k n)") for w in (w_in, w_hi, w_lo)]
        logit = x_room[:, 0:T].rearrange("p (h k) -> p h k", k=TOK)
        prob = x_room[:, T:3 * T].rearrange("p (u n) -> p u n", u=2)
        probT = x_room[:, 3 * T:3 * T + 2 * GROUPS * ROWS].rearrange("p (u g n) -> p u g n", u=2, g=GROUPS)
        rsum = sb("rsum", [P, 2, HEADS])
        attn = sb("attn", [P, 2, HEADS, HD])
        attnT_hi, attnT_lo = (w[:, 0:KD * T].rearrange("p (c n) -> p c n", c=KD) for w in w_room[1:])
        ln = w_room[0][:, 0:NT * DIM].rearrange("p (t n) -> p t n", t=NT)
        silu = w_room[0][:, 0:2 * COLS].rearrange("p (u n) -> p u n", u=2)
        hid = w_room[0][:, 2 * COLS:4 * COLS].rearrange("p (u n) -> p u n", u=2)
        res = h0

        ps = ctx.enter_context(nc.psum_tensor("ps", [P, 8, 512], f32))

        patch_in = [sem(f"patch_in{k}") for k in range(KP)]
        rows_loaded, wqk_loaded = sem("rows_loaded"), sem("wqk_loaded")
        wv_loaded, wp_loaded, tab_loaded = sem("wv_loaded"), sem("wp_loaded"), sem("tab_loaded")
        ffn_loaded = [sem(f"ffn_loaded{k}") for k in range(3)]
        ident_made, padded, ones_made = sem("ident_made"), sem("padded"), sem("ones_made")
        sel_hi_made, rows_lo_made = sem("sel_hi_made"), sem("rows_lo_made")
        patch_hi, patch_lo = sem("patch_hi"), sem("patch_lo")
        wqk_meaned, wqk_centred, wqk_hi_made, wqk_split = map(
            sem, ["wqk_meaned", "wqk_centred", "wqk_hi_made", "wqk_split"])
        wv_hi_made, wv_split, wp_split = sem("wv_hi_made"), sem("wv_split"), sem("wp_split")
        rope_made, tabs_step, beta_made = sem("rope_made"), sem("tabs_step"), sem("beta_made")
        embedded, h0_kept, stat_step, var_made, guess_step, newton_step, shift_made = map(
            sem, ["embedded", "h0_kept", "stat_step", "var_made", "guess_step", "newton_step", "shift_made"])
        normed, lnT_in, lnT_hi_made, lnT_split = map(
            sem, ["normed", "lnT_in", "lnT_hi_made", "lnT_split"])
        qk_in, squared, summed, hguess_step, hnewton_step = map(
            sem, ["qk_in", "squared", "summed", "hguess_step", "hnewton_step"])
        hvar_made, heads_cut = sem("hvar_made"), sem("heads_cut")
        parts_made, parts_added, roped = map(sem, ["parts_made", "parts_added", "roped"])
        qkT_in, q_ready, k_ready = sem("qkT_in"), sem("q_ready"), sem("k_ready")
        v_in, v_kept = sem("v_in"), sem("v_kept")
        v_spread = [sem(f"v_spread{p}") for p in range(PAIRS)]
        scored, topped, shifted, prob_made = map(sem, ["scored", "topped", "shifted", "prob_made"])
        probT_in, probT_kept, mixed, rsum_made, attn_made = map(
            sem, ["probT_in", "probT_kept", "mixed", "rsum_made", "attn_made"])
        attnT_in, attnT_hi_made, attnT_split = map(sem, ["attnT_in", "attnT_hi_made", "attnT_split"])
        projected, x1_made = sem("projected"), sem("x1_made")
        gate_in, up_in, silu_made, hid_made, hid_hi_made, hid_split = map(
            sem, ["gate_in", "up_in", "silu_made", "hid_made", "hid_hi_made", "hid_split"])
        down_in, res_made, stored = sem("down_in"), sem("res_made"), sem("stored")

        SCORE_BANK, PT_BANK, MIX_BANK = 0, 2, 4
        LN_BANK, QK_BANK, VT_BANK = 5, 6, 7
        GATE_BANK, UP_BANK = [2, 3], [0, 1]
        DOWN_BANK = [4, 5, 6, 7, 4]

        order = BEFORE + sum(BESIDE, []) + AFTER

        def ahead(stage, other):
            return sum(name == stage for name, _ in order[:order.index(other)])

        def tile_for(tokens):
            return -(-tokens // P)

        def spreads(p):
            for b in (2 * p, 2 * p + 1):
                for t in range(b * TOK // P, tile_for((b + 1) * TOK)):
                    lo, hi = max(b * TOK, t * P), min((b + 1) * TOK, t * P + P)
                    for r in range(REP):
                        yield b, t, r, lo, hi

        block = ctx.enter_context(nc.Block())

        @block.sync
        def _(sp):
            for k in range(KP):
                sp.dma_start(x_in[:, k, :], xT[:, k, :]).then_inc(patch_in[k], 16)
                if k == 0:
                    sp.dma_start(rows_in[:], tok_rows).then_inc(rows_loaded, 16)
                    sp.dma_start(sel_in[:], selT).then_inc(rows_loaded, 16)
            sp.dma_start(wqk_in[:], wqkT).then_inc(wqk_loaded, 16)
            sp.dma_start(tab_sb[:], tab).then_inc(tab_loaded, 16)
            sp.dma_start(gam[:], gammas).then_inc(tab_loaded, 16)
            sp.dma_start(bet[:], betas).then_inc(tab_loaded, 16)
            sp.dma_start(tabT_sb[:], tabT).then_inc(tab_loaded, 16)
            sp.dma_start(mask[:], maskT).then_inc(tab_loaded, 16)
            sp.dma_start(wv_in[:], wvT).then_inc(wv_loaded, 16)
            sp.dma_start(wp_in[:], wpT).then_inc(wp_loaded, 16)
            sp.dma_start(bp_in[:], b_proj).then_inc(wp_loaded, 16)
            sp.wait_ge(ones_made, 3)
            for p in range(PAIRS):
                sp.wait_ge(v_kept, 2 * tile_for(2 * (p + 1) * TOK))
                if p >= V_RING:
                    sp.wait_ge(mixed, p - V_RING + 1)
                for b, t, r, lo, hi in spreads(p):
                    k = r * TOK + lo - b * TOK
                    sp.dma_start(v_rep[k:k + hi - lo, p % V_RING, b % 2, r, :, :],
                                 v_tok[lo - t * P:hi - t * P, t, r, :, :]).then_inc(v_spread[p], 16)
            for t, (a, n) in enumerate(TILES):
                sp.wait_ge(res_made, t + 1)
                sp.dma_start(out[a:a + n, :], res[0:n, t, :]).then_inc(stored, 16)
            sp.wait_ge(stored, 16 * NT)

        @block.gpsimd
        def _(pool):
            nc.gpsimd.memset(ident[:], 0.0).then_inc(ident_made, 1)
            pool.wait_ge(ident_made, 1)
            nc.gpsimd.affine_select(out=ident[:], in_=ident[:], compare_op=ALU.not_equal, fill=1.0,
                                    base=0, pattern=[[-1, P]], channel_multiplier=1).then_inc(ident_made, 1)
            nc.gpsimd.memset(one_row_in[:], 1.0).then_inc(padded, 1)
            nc.gpsimd.memset(qT[:, :, T:T + 1], 0.0).then_inc(padded, 1)
            nc.gpsimd.memset(v_rep[:], 0.0).then_inc(ones_made, 1)
            nc.gpsimd.memset(v_tok[:, :, :, :, 0:HD], 0.0).then_inc(ones_made, 1)
            nc.gpsimd.memset(v_tok[:, :, :, :, HD:HV], 1.0).then_inc(ones_made, 1)
            pool.wait_ge(wv_hi_made, 1)
            nc.gpsimd.tensor_tensor(out=wv_lo[:], in0=wv_in[:], in1=wv_hi[:].bitcast(f32),
                                    op=ALU.subtract).then_inc(wv_split, 1)
            pool.wait_ge(tab_loaded, 80)
            nc.gpsimd.tensor_tensor(out=rope_a[:], in0=tab_sb[:, 0],
                                    in1=gam[:, None, 0].broadcast_to([P, NT, 2, HD]),
                                    op=ALU.mult).then_inc(rope_made, 1)
            nc.gpsimd.tensor_tensor(out=rope_b[:], in0=tab_sb[:, 1],
                                    in1=gam[:, None, 1].broadcast_to([P, NT, 2, HD]),
                                    op=ALU.mult).then_inc(rope_made, 1)
            for j in range(2):
                for w in range(2):
                    nc.gpsimd.tensor_scalar(bT[:, j, w, :], tabT_sb[:, j, w, :], bet[:, j, w:w + 1],
                                            None, ALU.mult).then_inc(tabs_step, 1)
            pool.wait_ge(tabs_step, 4)
            nc.gpsimd.tensor_tensor(out=betaT[:], in0=bT[:, 0], in1=bT[:, 1],
                                    op=ALU.add).then_inc(tabs_step, 1)
            pool.wait_ge(tabs_step, 5)
            nc.gpsimd.tensor_copy(beta_all[:], betaT[:, :, None, :].broadcast_to([P, 2, IMAGES, TOK])
                                  ).then_inc(beta_made, 1)

            def add_parts(t):
                n = TILES[t][1]
                pool.wait_ge(parts_made, 3 * (t + 1))
                nc.gpsimd.tensor_tensor(out=part_a[0:n, t % 2, :], in0=part_a[0:n, t % 2, :],
                                        in1=part_b[0:n, t % 2, :], op=ALU.add).then_inc(parts_added, 1)

            def split(hi, lo, src, semaphore, n0):
                nc.gpsimd.tensor_copy(hi, src).then_inc(semaphore, 1)
                pool.wait_ge(semaphore, n0 + 1)
                nc.gpsimd.tensor_tensor(out=lo, in0=src, in1=hi.bitcast(f32),
                                        op=ALU.subtract).then_inc(semaphore, 1)

            def cut_heads(p):
                pool.wait_ge(k_ready, tile_for(2 * (p + 1) * TOK))
                if p >= K_RING:
                    pool.wait_ge(scored, p - K_RING + 1)
                nc.gpsimd.tensor_tensor(
                    out=k_heads[:, p % K_RING],
                    in0=kT[:, :, None, 2 * p * TOK:2 * (p + 1) * TOK].broadcast_to([P, KD, CH, 2 * TOK]),
                    in1=mask[:, None, :, None].broadcast_to([P, KD, CH, 2 * TOK]),
                    op=ALU.mult).then_inc(heads_cut, 1)

            for k in range(KP):
                pool.wait_ge(patch_in[k], 32)
            pool.dma_start(wg[:], wgT).then_inc(ffn_loaded[0], 16)
            pool.dma_start(wu[:], wuT).then_inc(ffn_loaded[1], 16)
            pool.dma_start(wd[:], wdT).then_inc(ffn_loaded[2], 16)

            for kind, i in CUTS:
                if kind == "add":
                    add_parts(i)
                elif kind == "cut":
                    cut_heads(i)
                else:
                    pool.wait_ge(wp_loaded, 32)
                    split(wp_hi[:], wp_lo[:], wp_in[:], wp_split, 0)
                    split(bp_hi[:], bp_lo[:], bp_in[:], wp_split, 2)

        @block.scalar
        def _(act):
            nc.scalar.preload_act_table_set("natural_log_exp_and_others")
            for k in range(KP):
                act.dma_start(w_in[:, k, :], wT[:, k, :]).then_inc(patch_in[k], 16)
            for k in range(KP):
                act.wait_ge(patch_in[k], 32)
                nc.scalar.copy(x_hi[:, k, :], x_in[:, k, :]).then_inc(patch_hi, 1)
                nc.scalar.copy(w_hi[:, k, :], w_in[:, k, :]).then_inc(patch_hi, 1)
                if k == 0:
                    act.wait_ge(rows_loaded, 32)
                    nc.scalar.copy(rows_hi[:], rows_in[:]).then_inc(sel_hi_made, 1)
                    nc.scalar.copy(sel[:], sel_in[:]).then_inc(sel_hi_made, 1)
            act.wait_ge(padded, 2)
            nc.scalar.copy(one_row[:], one_row_in[:]).then_inc(sel_hi_made, 1)
            act.wait_ge(wv_loaded, 16)
            nc.scalar.copy(wv_hi[:], wv_in[:]).then_inc(wv_hi_made, 1)
            act.wait_ge(wqk_centred, 1)
            nc.scalar.copy(wqk_hi[:], wqk_in[:]).then_inc(wqk_hi_made, 1)

            def guess_rstd(which, t):
                n, i = TILES[t][1], which * NT + t
                act.wait_ge(var_made, i + 1)
                nc.scalar.activation(log_var[0:n, i:i + 1], var[0:n, i:i + 1], ACT.Ln).then_inc(guess_step, 1)
                act.wait_ge(guess_step, 2 * i + 1)
                nc.scalar.activation(guess[0:n, i:i + 1], log_var[0:n, i:i + 1], ACT.Exp, scale=-0.5
                                     ).then_inc(guess_step, 1)

            def apply_norm(which, t, src):
                n, i = TILES[t][1], which * NT + t
                act.wait_ge(shift_made, i + 1)
                nc.scalar.activation(ln[0:n, t, :], src, ACT.Identity, bias=shift[0:n, i:i + 1],
                                     scale=rstd[0:n, i:i + 1]).then_inc(normed, 1)

            def keep_h0(t):
                n = TILES[t][1]
                nc.scalar.copy(h0[0:n, t, :], ps[0:n, t, 0:DIM]).then_inc(h0_kept, 1)

            def lnT_upper(which, t):
                a, n = TILES[t]
                act.wait_ge(lnT_in, which * NT + t + 1)
                nc.scalar.copy(lnT_hi[:, :, a:a + n],
                               ps[:, LN_BANK, 0:KD * n].rearrange("p (c n) -> p c n", c=KD)
                               ).then_inc(lnT_hi_made, 1)

            def squares_and_values(t):
                n = TILES[t][1]
                act.wait_ge(qk_in, t + 1)
                if t >= 2:
                    act.wait_ge(summed, t - 1)
                nc.scalar.activation(square[0:n, t % 2, :], ps[0:n, QK_BANK, :], ACT.Square
                                     ).then_inc(squared, 1)
                act.wait_ge(v_in, t + 1)
                if t == 0:
                    act.wait_ge(ones_made, 3)
                for r0, r1, g, c0, c1 in ((0, 2, 5, 0, 160), (2, 3, 6, 160, 256)):
                    nc.scalar.copy(v_tok[0:n, t, r0:r1, 0:g, 0:HD],
                                   ps[0:n, VT_BANK, c0:c1].rearrange("p (r g d) -> p r g d", g=g, d=HD)
                                   ).then_inc(v_kept, 1)

            def guess_heads(t):
                n = TILES[t][1]
                act.wait_ge(hvar_made, t + 1)
                nc.scalar.activation(hlog[0:n, t, :], hvar[0:n, t, :], ACT.Ln).then_inc(hguess_step, 1)
                act.wait_ge(hguess_step, 2 * t + 1)
                nc.scalar.activation(hguess[0:n, t, :], hlog[0:n, t, :], ACT.Exp, scale=-0.5
                                     ).then_inc(hguess_step, 1)

            def beside(stages):
                for stage, t in stages:
                    if stage == "norm1":
                        lnT_upper(0, t)
                    elif stage == "qkv":
                        squares_and_values(t)
                    elif stage == "rms":
                        guess_heads(t)
                    elif stage == "embed":
                        guess_rstd(0, t)
                    elif stage == "scale":
                        apply_norm(0, t, ps[0:TILES[t][1], t, 0:DIM])
                        keep_h0(t)
                    elif stage == "proj":
                        guess_rstd(1, t)
                    elif stage == "scale2":
                        apply_norm(1, t, x1[0:TILES[t][1], t, :])
                    elif stage == "norm2":
                        lnT_upper(1, t)

            def exponentials(p):
                act.wait_ge(shifted, p + 1)
                if p >= 2:
                    act.wait_ge(probT_in, 2 * (p - 1))
                nc.scalar.activation(prob[0:ROWS, p % 2, :], logit[0:ROWS].rearrange("p h k -> p (h k)"),
                                     ACT.Exp).then_inc(prob_made, 1)

            def attnT_upper(p):
                act.wait_ge(attnT_in, p + 1)
                for j in range(2):
                    nc.scalar.copy(attnT_hi[:, :, (2 * p + j) * TOK:(2 * p + j + 1) * TOK],
                                   ps[:, MIX_BANK, 0:KD * ROWS].rearrange("p (c n) -> p c n", c=KD)
                                   [:, :, 64 * j:64 * j + TOK]).then_inc(attnT_hi_made, 1)

            def keep_probT(p):
                if p >= 2:
                    act.wait_ge(mixed, p - 1)
                for i in range(2):
                    act.wait_ge(probT_in, 2 * p + i + 1)
                    nc.scalar.copy(probT[0:REP * TOK, p % 2, 3 * i:3 * i + 3, :],
                                   ps[0:REP * TOK, PT_BANK + i, 0:3 * ROWS].rearrange("p (g n) -> p g n", g=3)
                                   ).then_inc(probT_kept, 1)

            beside(BEFORE)
            exponentials(0)
            for p in range(PAIRS):
                if p >= 1:
                    attnT_upper(p - 1)
                keep_probT(p)
                if p + 1 < PAIRS:
                    exponentials(p + 1)
                beside(BESIDE[p])
            attnT_upper(PAIRS - 1)
            beside(AFTER)

            def hidden_upper(u):
                half, j = divmod(u, KH)
                act.wait_ge(hid_made, u + 1)
                nc.scalar.copy(hid_hi[:, j, half * COLS:(half + 1) * COLS], hid[:, u % 2, :]
                               ).then_inc(hid_hi_made, 1)

            for u in range(2 * KH):
                act.wait_ge(gate_in, u + 1)
                if u >= 2:
                    act.wait_ge(hid_made, u - 1)
                nc.scalar.activation(silu[:, u % 2, :], ps[:, GATE_BANK[u % 2], 0:COLS], ACT.Silu,
                                     scale=CODE_SCALE).then_inc(silu_made, 1)
                if u >= 1:
                    hidden_upper(u - 1)
            hidden_upper(2 * KH - 1)

        @block.vector
        def _(dve):
            for k in range(KP):
                dve.wait_ge(patch_hi, 2 * k + 1)
                nc.vector.tensor_tensor(out=x_lo[:, k, :], in0=x_in[:, k, :],
                                        in1=x_hi[:, k, :].bitcast(f32), op=ALU.subtract
                                        ).then_inc(patch_lo, 1)
                dve.wait_ge(patch_hi, 2 * k + 2)
                nc.vector.tensor_tensor(out=w_lo[:, k, :], in0=w_in[:, k, :],
                                        in1=w_hi[:, k, :].bitcast(f32), op=ALU.subtract
                                        ).then_inc(patch_lo, 1)
                if k == 0:
                    dve.wait_ge(sel_hi_made, 2)
                    nc.vector.tensor_tensor(out=rows_lo[:], in0=rows_in[:], in1=rows_hi[:].bitcast(f32),
                                            op=ALU.subtract).then_inc(rows_lo_made, 1)
            dve.wait_ge(wqk_loaded, 16)
            wqk_heads = wqk_in[:].rearrange("p c (h d) -> p (c h) d", d=HD)
            means = wqk_mean[:].rearrange("p c h -> p (c h)")
            nc.vector.tensor_reduce(means, wqk_heads, AX.X, ALU.add).then_inc(wqk_meaned, 1)
            dve.wait_ge(wqk_meaned, 1)
            nc.vector.tensor_scalar(means, means, 1.0 / HD, None, ALU.mult).then_inc(wqk_meaned, 1)
            dve.wait_ge(wqk_meaned, 2)
            nc.vector.tensor_tensor(out=wqk_heads, in0=wqk_heads,
                                    in1=means[:, :, None].broadcast_to([P, KD * 2 * HEADS, HD]),
                                    op=ALU.subtract).then_inc(wqk_centred, 1)
            dve.wait_ge(wqk_hi_made, 1)
            nc.vector.tensor_tensor(out=wqk_lo[:], in0=wqk_in[:], in1=wqk_hi[:].bitcast(f32),
                                    op=ALU.subtract).then_inc(wqk_split, 1)

            def moments(which, t, src):
                n, i = TILES[t][1], which * NT + t
                nc.vector.bn_stats(stats[0:n, which, t, :], src).then_inc(stat_step, 1)
                dve.wait_ge(stat_step, 2 * i + 1)
                nc.vector.bn_aggr(mv[0:n, which, t, :], stats[0:n, which, t, :]).then_inc(stat_step, 1)
                dve.wait_ge(stat_step, 2 * i + 2)
                nc.vector.tensor_scalar(var[0:n, i:i + 1], mv[0:n, which, t, 1:2], EPS, None, ALU.add
                                        ).then_inc(var_made, 1)

            def norm_scale(which, t):
                n, i = TILES[t][1], which * NT + t
                v, y, z, r = (a[0:n, i:i + 1] for a in (var, guess, newton, rstd))
                dve.wait_ge(guess_step, 2 * i + 2)
                nc.vector.tensor_tensor(out=z, in0=y, in1=y, op=ALU.mult).then_inc(newton_step, 1)
                dve.wait_ge(newton_step, 3 * i + 1)
                nc.vector.scalar_tensor_tensor(out=z, in0=z, scalar=-0.5, in1=v, op0=ALU.mult, op1=ALU.mult
                                               ).then_inc(newton_step, 1)
                dve.wait_ge(newton_step, 3 * i + 2)
                nc.vector.scalar_tensor_tensor(out=r, in0=z, scalar=1.5, in1=y,
                                               op0=ALU.add, op1=ALU.mult).then_inc(newton_step, 1)
                dve.wait_ge(newton_step, 3 * i + 3)
                nc.vector.scalar_tensor_tensor(out=shift[0:n, i:i + 1], in0=mv[0:n, which, t, 0:1],
                                               scalar=-1.0, in1=r, op0=ALU.mult,
                                               op1=ALU.mult).then_inc(shift_made, 1)

            def lnT_lower(which, t):
                a, n = TILES[t]
                dve.wait_ge(lnT_hi_made, which * NT + t + 1)
                nc.vector.tensor_tensor(out=lnT_lo[:, :, a:a + n],
                                        in0=ps[:, LN_BANK, 0:KD * n].rearrange("p (c n) -> p c n", c=KD),
                                        in1=lnT_hi[:, :, a:a + n].bitcast(f32), op=ALU.subtract
                                        ).then_inc(lnT_split, 1)

            def rope_parts(t):
                n = TILES[t][1]
                dve.wait_ge(squared, t + 1)
                if t == 0:
                    dve.wait_ge(rope_made, 2)
                if t >= 2:
                    dve.wait_ge(roped, t - 1)
                x = ps[0:n, QK_BANK, :].rearrange("p (w h d) -> p w h d", w=2, d=HD)
                a = part_a[0:n, t % 2, :].rearrange("p (w h d) -> p w h d", w=2, d=HD)
                b = part_b[0:n, t % 2, :].rearrange("p (w h d) -> p w h d", w=2, d=HD)
                nc.vector.tensor_reduce(ssum[0:n, t, :],
                                        square[0:n, t % 2, :].rearrange("p (h d) -> p h d", d=HD),
                                        AX.X, ALU.add).then_inc(summed, 1)
                nc.vector.tensor_tensor(out=a, in0=x,
                                        in1=rope_a[0:n, t, :, None].broadcast_to([n, 2, HEADS, HD]),
                                        op=ALU.mult).then_inc(parts_made, 1)
                dve.wait_ge(summed, t + 1)
                nc.vector.tensor_scalar(hvar[0:n, t, :], ssum[0:n, t, :], 1.0 / HD, EPS_HEAD, ALU.mult, ALU.add
                                        ).then_inc(hvar_made, 1)
                for s in range(2):
                    o, i = slice(s * HALF, (s + 1) * HALF), slice((1 - s) * HALF, (2 - s) * HALF)
                    nc.vector.tensor_tensor(out=b[:, :, :, o], in0=x[:, :, :, i],
                                            in1=rope_b[0:n, t, :, None, o].broadcast_to([n, 2, HEADS, HALF]),
                                            op=ALU.mult).then_inc(parts_made, 1)

            def scale_heads(t):
                n = TILES[t][1]
                v, y, z, r = (a[0:n, t, :] for a in (hvar, hguess, hnewton, hrstd))
                dve.wait_ge(hguess_step, 2 * t + 2)
                nc.vector.tensor_tensor(out=z, in0=y, in1=y, op=ALU.mult).then_inc(hnewton_step, 1)
                dve.wait_ge(hnewton_step, 3 * t + 1)
                nc.vector.scalar_tensor_tensor(out=z, in0=z, scalar=-0.5, in1=v, op0=ALU.mult, op1=ALU.mult
                                               ).then_inc(hnewton_step, 1)
                dve.wait_ge(hnewton_step, 3 * t + 2)
                nc.vector.scalar_tensor_tensor(out=r, in0=z, scalar=1.5, in1=y, op0=ALU.add, op1=ALU.mult
                                               ).then_inc(hnewton_step, 1)
                dve.wait_ge(hnewton_step, 3 * t + 3)
                dve.wait_ge(parts_added, t + 1)
                if t >= 2:
                    dve.wait_ge(qkT_in, t - 1)
                nc.vector.tensor_tensor(
                    out=qk[0:n, t % 2, :].rearrange("p (h d) -> p h d", d=HD),
                    in0=part_a[0:n, t % 2, :].rearrange("p (h d) -> p h d", d=HD),
                    in1=r[:, :, None].broadcast_to([n, 2 * HEADS, HD]),
                    op=ALU.mult).then_inc(roped, 1)

            def keep_qkT(t):
                a, n = TILES[t]
                dve.wait_ge(qkT_in, t + 1)
                if t == 0:
                    dve.wait_ge(beta_made, 1)
                src = ps[:, VT_BANK, 0:4 * n].rearrange("p (w c n) -> p w c n", w=2, c=KD)
                beta = beta_all[:].rearrange("p w b k -> p w (b k)")
                for w, (dst, ready) in enumerate(((qT, q_ready), (kT, k_ready))):
                    nc.vector.tensor_tensor(out=dst[:, :, a:a + n], in0=src[:, w],
                                            in1=beta[:, w:w + 1, a:a + n].broadcast_to([P, KD, n]),
                                            op=ALU.add).then_inc(ready, 1)

            def residual(t):
                n = TILES[t][1]
                dve.wait_ge(projected, t + 1)
                if t == 0:
                    dve.wait_ge(h0_kept, NT)
                nc.vector.tensor_tensor(out=x1[0:n, t, :], in0=ps[0:n, QK_BANK, 0:DIM], in1=h0[0:n, t, :],
                                        op=ALU.add).then_inc(x1_made, 1)
                dve.wait_ge(x1_made, t + 1)
                moments(1, t, x1[0:n, t, :])

            def beside(stages):
                for stage, t in stages:
                    if stage == "embed":
                        dve.wait_ge(embedded, t + 1)
                        moments(0, t, ps[0:TILES[t][1], t, 0:DIM])
                    elif stage == "scale":
                        norm_scale(0, t)
                    elif stage == "scale2":
                        norm_scale(1, t)
                    elif stage == "norm1":
                        lnT_lower(0, t)
                    elif stage == "qkv":
                        rope_parts(t)
                    elif stage == "rms":
                        scale_heads(t)
                    elif stage == "rope":
                        keep_qkT(t)
                    elif stage == "proj":
                        residual(t)
                    elif stage == "norm2":
                        lnT_lower(1, t)

            def take_top(p):
                dve.wait_ge(scored, p + 1)
                s = ps[0:ROWS, SCORE_BANK:SCORE_BANK + KD, 0:CH * TOK].rearrange("p c (h k) -> p c h k", k=TOK)
                tops = top[0:ROWS, p % 2, :].rearrange("p (c h) -> p c h", c=KD)
                nc.vector.tensor_reduce(tops, s, AX.X, ALU.max).then_inc(topped, 1)
                dve.wait_ge(topped, p + 1)
                if p >= 1:
                    dve.wait_ge(prob_made, p)
                nc.vector.tensor_tensor(out=logit[0:ROWS].rearrange("p (c h) k -> p c h k", c=KD), in0=s,
                                        in1=tops[:, :, :, None].broadcast_to([ROWS, KD, CH, TOK]),
                                        op=ALU.subtract).then_inc(shifted, 1)

            def normalise(p):
                dve.wait_ge(mixed, p + 1)
                o = ps[0:ROWS, MIX_BANK, 0:HEADS * HV].rearrange("p (h d) -> p h d", d=HV)
                nc.vector.reciprocal(rsum[0:ROWS, p % 2, :], o[:, :, HD]).then_inc(rsum_made, 1)
                dve.wait_ge(rsum_made, p + 1)
                if p >= 2:
                    dve.wait_ge(attnT_in, p - 1)
                nc.vector.tensor_tensor(out=attn[0:ROWS, p % 2], in0=o[:, :, 0:HD],
                                        in1=rsum[0:ROWS, p % 2, :, None].broadcast_to([ROWS, HEADS, HD]),
                                        op=ALU.mult).then_inc(attn_made, 1)

            def attnT_lower(p):
                dve.wait_ge(attnT_hi_made, 2 * p + 2)
                for j in range(2):
                    cols = slice((2 * p + j) * TOK, (2 * p + j + 1) * TOK)
                    nc.vector.tensor_tensor(
                        out=attnT_lo[:, :, cols],
                        in0=ps[:, MIX_BANK, 0:KD * ROWS].rearrange("p (c n) -> p c n", c=KD)
                        [:, :, 64 * j:64 * j + TOK],
                        in1=attnT_hi[:, :, cols].bitcast(f32), op=ALU.subtract).then_inc(attnT_split, 1)

            beside(BEFORE)
            take_top(0)
            for p in range(PAIRS):
                if p + 1 < PAIRS:
                    take_top(p + 1)
                if p >= 1:
                    attnT_lower(p - 1)
                beside(BESIDE[p])
                normalise(p)
            attnT_lower(PAIRS - 1)
            beside(AFTER)

            def hidden_lower(u):
                half, j = divmod(u, KH)
                cols = slice(half * COLS, (half + 1) * COLS)
                dve.wait_ge(hid_hi_made, u + 1)
                nc.vector.tensor_tensor(out=hid_lo[:, j, cols], in0=hid[:, u % 2, :],
                                        in1=hid_hi[:, j, cols].bitcast(f32), op=ALU.subtract
                                        ).then_inc(hid_split, 1)

            def result(t):
                n = TILES[t][1]
                dve.wait_ge(down_in, t + 1)
                nc.vector.scalar_tensor_tensor(out=res[0:n, t, :], in0=ps[0:n, DOWN_BANK[t], 0:DIM],
                                               scalar=CODE_SCALE, in1=x1[0:n, t, :],
                                               op0=ALU.mult, op1=ALU.add).then_inc(res_made, 1)

            for u in range(2 * KH):
                dve.wait_ge(silu_made, u + 1)
                dve.wait_ge(up_in, u + 1)
                if u >= 2:
                    dve.wait_ge(hid_split, u - 1)
                nc.vector.scalar_tensor_tensor(out=hid[:, u % 2, :], in0=ps[:, UP_BANK[u % 2], 0:COLS],
                                               scalar=CODE_SCALE, in1=silu[:, u % 2, :],
                                               op0=ALU.mult, op1=ALU.mult).then_inc(hid_made, 1)
                if u >= 1:
                    hidden_lower(u - 1)
                if u >= KH + 2 and u < KH + 4:
                    result(u - KH - 2)
            hidden_lower(2 * KH - 1)
            for t in range(2, NT):
                result(t)

        @block.tensor
        def _(pe):
            def split_product(dst, steps, first=True, last=True):
                for i, (lhs, rhs) in enumerate(steps):
                    m = nc.tensor.matmul(dst, lhs, rhs, start=first and i == 0,
                                         stop=last and i == len(steps) - 1)
                return m

            def embed(t, k):
                a, n = TILES[t]
                pe.wait_ge(patch_hi, 2 * k + 2)
                pe.wait_ge(patch_lo, 2 * k + 2)
                split_product(ps[0:n, t, 0:DIM],
                              [(x_hi[:, k, a:a + n], w_hi[:, k, :]), (x_hi[:, k, a:a + n], w_lo[:, k, :]),
                               (x_lo[:, k, a:a + n], w_hi[:, k, :])], k == 0, False)

            def finish_embedding(t):
                a, n = TILES[t]
                for k in range(EARLY, KP):
                    embed(t, k)
                pe.wait_ge(rows_lo_made, 1)
                split_product(ps[0:n, t, 0:DIM], [(sel[:, a:a + n], rows_hi[:]), (sel[:, a:a + n], rows_lo[:])],
                              False, True).then_inc(embedded, 1)

            for k in range(EARLY):
                for t in range(NT):
                    embed(t, k)

            def transpose_ln(which, t):
                n, i = TILES[t][1], which * NT + t
                pe.wait_ge(normed, i + 1)
                if i == 0:
                    pe.wait_ge(ident_made, 2)
                if i >= 1:
                    pe.wait_ge(lnT_split, i)
                for c in range(KD):
                    m = nc.tensor.transpose(ps[:, LN_BANK, c * n:(c + 1) * n],
                                            ln[0:n, t, c * P:(c + 1) * P], ident[0:n, 0:n])
                m.then_inc(lnT_in, 1)

            def project_qkv(t):
                a, n = TILES[t]
                pe.wait_ge(lnT_split, t + 1)
                if t == 0:
                    pe.wait_ge(wqk_split, 1)
                    pe.wait_ge(wv_split, 1)
                else:
                    pe.wait_ge(parts_made, 3 * t)
                both = [(w, c) for w in range(3) for c in range(KD)]
                lhs = [lnT_hi, lnT_hi, lnT_lo]
                split_product(ps[0:n, QK_BANK, :],
                              [(lhs[w][:, c, a:a + n], [wqk_hi, wqk_lo, wqk_hi][w][:, c, :]) for w, c in both]
                              ).then_inc(qk_in, 1)
                if t >= 1:
                    pe.wait_ge(v_kept, 2 * t)
                if ahead("rope", ("qkv", t)):
                    pe.wait_ge(k_ready, ahead("rope", ("qkv", t)))
                split_product(ps[0:n, VT_BANK, 0:DIM],
                              [(lhs[w][:, c, a:a + n], [wv_hi, wv_lo, wv_hi][w][:, c, :]) for w, c in both]
                              ).then_inc(v_in, 1)

            def transpose_qk(t):
                n = TILES[t][1]
                pe.wait_ge(roped, t + 1)
                pe.wait_ge(v_kept, 2 * ahead("qkv", ("rope", t)))
                if t >= 1:
                    pe.wait_ge(k_ready, t)
                for w in range(4):
                    m = nc.tensor.transpose(ps[:, VT_BANK, w * n:(w + 1) * n],
                                            qk[0:n, t % 2, w * P:(w + 1) * P], ident[0:n, 0:n])
                m.then_inc(qkT_in, 1)

            def project_out(t):
                a, n = TILES[t]
                pe.wait_ge(attnT_split, 2 * min(PAIRS, -(-(a + n) // (2 * TOK))))
                if t == 0:
                    pe.wait_ge(wp_split, 4)
                    pe.wait_ge(sel_hi_made, 3)
                    pe.wait_ge(parts_made, 3 * NT)
                else:
                    pe.wait_ge(x1_made, t)
                steps = [(one_row[:, 0:n], bp_hi[:]), (one_row[:, 0:n], bp_lo[:])]
                for c in range(KD):
                    steps += [(attnT_hi[:, c, a:a + n], wp_hi[:, c, :]), (attnT_hi[:, c, a:a + n], wp_lo[:, c, :]),
                              (attnT_lo[:, c, a:a + n], wp_hi[:, c, :])]
                split_product(ps[0:n, QK_BANK, 0:DIM], steps).then_inc(projected, 1)

            def beside(stages):
                for stage, t in stages:
                    if stage == "embed":
                        finish_embedding(t)
                    elif stage == "norm1":
                        transpose_ln(0, t)
                    elif stage == "qkv":
                        project_qkv(t)
                    elif stage == "rope":
                        transpose_qk(t)
                    elif stage == "proj":
                        project_out(t)
                    elif stage == "norm2":
                        transpose_ln(1, t)

            def score(p):
                pe.wait_ge(heads_cut, p + 1)
                pe.wait_ge(q_ready, tile_for(min(T, (2 * p + 1) * TOK + WIDE[1])))
                if p == 0:
                    pe.wait_ge(padded, 2)
                    pe.wait_ge(normed, NT)
                    pe.wait_ge(h0_kept, NT)
                else:
                    pe.wait_ge(shifted, p)
                for j in range(2):
                    a = (2 * p + j) * TOK
                    for c in range(KD):
                        m = nc.tensor.matmul(ps[64 * j:64 * j + WIDE[j], SCORE_BANK + c, 0:CH * TOK],
                                             qT[:, c, a:a + WIDE[j]],
                                             k_heads[:, p % K_RING, c, :, j * TOK:(j + 1) * TOK],
                                             start=True, stop=True)
                m.then_inc(scored, 1)

            def transpose_prob(p):
                pe.wait_ge(prob_made, p + 1)
                for g in range(GROUPS):
                    if p >= 1 and g % 3 == 0:
                        pe.wait_ge(probT_kept, 2 * (p - 1) + g // 3 + 1)
                    a = GROUP_HEAD[g] * TOK
                    m = nc.tensor.transpose(ps[0:REP * TOK, PT_BANK + g // 3, (g % 3) * ROWS:(g % 3 + 1) * ROWS],
                                            prob[0:ROWS, p % 2, a:a + REP * TOK], ident[0:ROWS, 0:ROWS])
                    if g % 3 == 2:
                        m.then_inc(probT_in, 1)

            def mix(p):
                pe.wait_ge(probT_kept, 2 * (p + 1))
                pe.wait_ge(v_spread[p], 16 * len(list(spreads(p))))
                if p >= 1:
                    pe.wait_ge(attnT_split, 2 * p)
                for j in range(2):
                    q = slice(64 * j, 64 * j + WIDE[j])
                    for g in range(GROUPS):
                        if g < GROUPS - 1:
                            cols = slice(g * REP * HV, (g + 1) * REP * HV)
                            v = v_rep[0:REP * TOK, p % V_RING, j, :, g, :]
                        else:
                            cols = slice(15 * HV, 16 * HV)
                            v = v_rep[0:REP * TOK, p % V_RING, j, REP - 1, g, :]
                        m = nc.tensor.matmul(ps[q, MIX_BANK, cols], probT[0:REP * TOK, p % 2, g, q], v,
                                             start=True, stop=True)
                m.then_inc(mixed, 1)

            def transpose_attn(p):
                pe.wait_ge(attn_made, p + 1)
                flat = attn[0:ROWS, p % 2].rearrange("p h d -> p (h d)")
                for c in range(KD):
                    m = nc.tensor.transpose(ps[:, MIX_BANK, c * ROWS:(c + 1) * ROWS],
                                            flat[:, c * P:(c + 1) * P], ident[0:ROWS, 0:ROWS])
                m.then_inc(attnT_in, 1)

            beside(BEFORE)
            score(0)
            for p in range(PAIRS):
                if p + 1 < PAIRS:
                    score(p + 1)
                if p >= 1:
                    transpose_attn(p - 1)
                transpose_prob(p)
                beside(BESIDE[p])
                mix(p)
            transpose_attn(PAIRS - 1)
            beside(AFTER)

            for k in range(3):
                pe.wait_ge(ffn_loaded[k], 16)
            pe.wait_ge(probT_kept, 2 * PAIRS)
            pe.wait_ge(shifted, PAIRS)

            def gate_up(u):
                half, j = divmod(u, KH)
                pe.wait_ge(lnT_split, NT + tile_for((half + 1) * COLS))
                cols, units = slice(half * COLS, (half + 1) * COLS), slice(j * P, (j + 1) * P)
                if u >= 2:
                    pe.wait_ge(silu_made, u - 1)
                split_product(ps[:, GATE_BANK[u % 2], 0:COLS],
                              [(wg[:, c, units], x[:, c, cols]) for c in range(KD) for x in (lnT_hi, lnT_lo)]
                              ).then_inc(gate_in, 1)
                if u >= 2:
                    pe.wait_ge(hid_made, u - 1)
                split_product(ps[:, UP_BANK[u % 2], 0:COLS],
                              [(wu[:, c, units], x[:, c, cols]) for c in range(KD) for x in (lnT_hi, lnT_lo)]
                              ).then_inc(up_in, 1)

            def down(t):
                a, n = TILES[t]
                pe.wait_ge(hid_split, KH * (1 if a + n <= COLS else 2))
                if t == 0:
                    pe.wait_ge(attnT_split, 2 * PAIRS)
                    pe.wait_ge(lnT_split, 2 * NT)
                    pe.wait_ge(x1_made, NT)
                if t == 4:
                    pe.wait_ge(res_made, 1)
                split_product(ps[0:n, DOWN_BANK[t], 0:DIM],
                              [(h[:, j, a:a + n], wd[:, j, :]) for j in range(KH) for h in (hid_hi, hid_lo)]
                              ).then_inc(down_in, 1)

            for u in range(2 * KH):
                gate_up(u)
                if u >= KH + 1 and u < KH + 3:
                    down(u - KH - 1)
            for t in range(2, NT):
                down(t)


def _chunks(a):
    k = a.shape[0] // P
    return np.ascontiguousarray(a.reshape(k, P, -1).transpose(1, 0, 2))


def _rotary():
    inv = (1.0 / np.float32(10000.0) ** (np.arange(HALF, dtype=np.float32) / np.float32(HALF))).astype(np.float32)
    freq = np.outer(np.arange(TOK, dtype=np.float32), inv).astype(np.float32)
    cos = np.cos(np.concatenate([freq, freq], -1))
    sin = np.sin(np.concatenate([-freq, freq], -1))
    scale = np.float32(HD ** -0.5)
    return np.stack([np.stack([cos * scale, cos]), np.stack([sin * scale, sin])]).astype(np.float32)


def kernel(x, L0_tok_W, L0_tok_b, L0_tok_cls_token, L0_tok_pos_embed, L0_attn_w_qkv, L0_attn_w_proj,
           L0_attn_b_proj, L0_attn_q_gamma, L0_attn_q_beta, L0_attn_k_gamma, L0_attn_k_beta,
           L0_ffn_w_gate, L0_ffn_w_up, L0_ffn_w_down):
    import concourse.bacc as bacc
    from concourse.bass_utils import run_bass_kernel_spmd

    x = np.asarray(x)
    f = np.float32
    patches = x.reshape(IMAGES, CHANNELS, GRID, PATCH, GRID, PATCH).transpose(1, 3, 5, 0, 2, 4)
    cols = np.zeros((PATCH_DIM, IMAGES, TOK), f)
    cols[:, :, 1:] = patches.reshape(PATCH_DIM, IMAGES, TOK - 1)
    sel = np.zeros((TOK + 2, IMAGES, TOK), f)
    for k in range(TOK):
        sel[k, :, k] = 1
    sel[TOK, :, 1:] = 1
    sel[TOK + 1, :, 0] = 1
    tok_rows = np.concatenate([np.asarray(L0_tok_pos_embed).reshape(TOK, DIM), np.asarray(L0_tok_b).reshape(1, DIM),
                               np.asarray(L0_tok_cls_token).reshape(1, DIM)])
    w_qkv, w_proj = np.asarray(L0_attn_w_qkv), np.asarray(L0_attn_w_proj)
    heads = np.arange(DIM).reshape(HEADS, HD)
    v_rows = np.concatenate([heads[h] for group in VALUE_HEADS for h in group])
    rot = _rotary()
    pos = np.arange(NT * P) % TOK
    tab = rot[:, :, pos, :].reshape(2, 2, NT, P, HD).transpose(3, 0, 2, 1, 4)
    tabT = np.tile(rot.transpose(3, 0, 1, 2), (P // HD, 1, 1, 1))
    swap = np.r_[HALF:HD, 0:HALF]
    g = [np.asarray(L0_attn_q_gamma), np.asarray(L0_attn_k_gamma)]
    b = [np.asarray(L0_attn_q_beta), np.asarray(L0_attn_k_beta)]
    gammas = np.broadcast_to(np.stack([np.stack(g), np.stack([v[swap] for v in g])]), (P, 2, 2, HD))
    betas = np.tile(np.stack([np.stack(b, -1), np.stack([v[swap] for v in b], -1)], 1), (P // HD, 1, 1))

    arrays = {
        "xT": _chunks(cols.reshape(PATCH_DIM, T)),
        "wT": _chunks(np.asarray(L0_tok_W).T),
        "selT": sel.reshape(TOK + 2, T),
        "tok_rows": tok_rows,
        "wqkT": _chunks(w_qkv[:2 * DIM].T),
        "wvT": _chunks(w_qkv[2 * DIM:][v_rows].T),
        "wpT": _chunks(w_proj.T),
        "b_proj": np.asarray(L0_attn_b_proj).reshape(1, DIM),
        "gammas": gammas,
        "betas": betas,
        "tab": tab,
        "tabT": tabT,
        "maskT": np.repeat(np.eye(CH, dtype=f), HD, axis=0),
        "wgT": _chunks(np.asarray(L0_ffn_w_gate).T),
        "wuT": _chunks(np.asarray(L0_ffn_w_up).T),
        "wdT": _chunks(np.asarray(L0_ffn_w_down).T),
    }
    nc = bacc.Bacc("TRN2", target_bir_lowering=False, num_devices=1)
    given, args = {}, {}
    for name, a in arrays.items():
        a = np.ascontiguousarray(a)
        given[f"in_{name}"] = a
        args[name] = nc.dram_tensor(f"in_{name}", a.shape, mybir.dt.from_np(a.dtype), kind="ExternalInput").ap()
    out = nc.dram_tensor("out", (T, DIM), mybir.dt.float32, kind="ExternalOutput").ap()
    build(nc, out=out, **args)
    r = run_bass_kernel_spmd(nc, [given], core_ids=[0])
    return r.results[0]["out"].reshape(IMAGES, TOK, DIM)
```

```python
import math
from contextlib import ExitStack

import numpy as np

import concourse.bass as bass
from concourse import mybir

IMAGES, CHANNELS, SIDE, PATCH = 16, 3, 96, 16
GRID = SIDE // PATCH
TOK = GRID * GRID + 1
T = IMAGES * TOK
P = 128
DIM, HEADS, HD, HIDDEN = 256, 16, 16, 768
HALF = HD // 2
PATCH_DIM = CHANNELS * PATCH * PATCH
KP = PATCH_DIM // P
KD = DIM // P
KH = HIDDEN // P
TILES = [(a, min(P, T - a)) for a in range(0, T, P)]
NT = len(TILES)
PAIRS = IMAGES // 2
COLS = T // 2
EPS, EPS_HEAD = 1e-5, 1e-6
GUESS, GUESS_HEAD = 0.5 ** (1 / 3), (0.5 / HD) ** (1 / 3)
CODE_SCALE = 1.0 / 127.0

CH = P // HD
REP = 3
GROUPS = 6
GROUP_HEAD = [0, 3, 6, 9, 12, 13]
VALUE_HEADS = [[3 * g + r for g in range(5)] + ([15] if r == 2 else []) for r in range(REP)]
HV = HD + 2
WIDE = [64, TOK + 1]
ROWS = 64 + WIDE[1]
V_RING, K_RING = 3, 3

def _order(text):
    return [(w.rstrip("0123456789"), int(w[len(w.rstrip("0123456789")):])) for w in text.split()]


PE_ORDER = _order("""
embed0 embed1 embed2 embed3 norm0 embed4 qk0 v0 norm1 norm2 qk1 v1 rope0 norm3 qk2 v2 rope1 score0 v3
norm4 score1 probT0 qk3 score2 rope2 probT1 mix0 mix1 attnT0 probT2 v4 score3 mix2 qk4 probT3 rope3 attnT1
mix3 score4 attnT2 proj0 probT4 rope4 score5 mix4 attnT3 score6 probT5 proj1 mix5 attnT4 renorm0 score7
probT6 attnT5 mix6 proj2 attnT6 probT7 renorm1 mix7 proj3 attnT7 renorm2 proj4 renorm3 ffn0 ffn1 ffn2 ffn3
renorm4 ffn4 ffn5 ffn6 ffn7 ffn8 down0 down1 ffn9 ffn10 ffn11 step0 step1 step2 step3 step4 step5""")
ACT_ORDER = _order("""
embed0 wqk0 scale0 norm0 embed1 embed2 embed3 qk0 scale1 norm1 scale2 v0 rms0 norm2 keep0 qk1 scale3 v1
embed4 rms1 norm3 keep1 qk2 v2 keep2 scale4 keep3 keep4 exp0 norm4 v3 rms2 probT0 exp1 qk3 probT1 exp2
attnT0 rms3 probT2 v4 exp3 qk4 probT3 rms4 attnT1 attnT2 exp4 probT4 attnT3 proj0 exp5 probT5 rescale0
attnT4 exp6 renorm0 proj1 probT6 attnT5 exp7 rescale1 attnT6 probT7 proj2 renorm1 rescale2 attnT7 renorm2
proj3 rescale3 proj4 gate0 gate1 rescale4 hid0 renorm3 hid1 gate2 gate3 hid2 renorm4 hid3 gate4 gate5 hid4
hid5 gate6 gate7 hid6 gate8 hid7 gate9 hid8 gate10 gate11 hid9 hid10 hid11""")
DVE_ORDER = _order("""
centre0 embed0 embed1 newton0 scale0 embed2 wqk0 norm0 embed3 embed4 newton1 newton2 scale1 scale2 newton3
parts0 norm1 squares0 add0 scale3 rootms0 norm2 rms0 parts1 squares1 rope0 rootms1 rms1 newton4 norm3
scale4 rope1 squares2 top0 parts2 norm4 top1 rootms2 rms2 top2 rope2 mix0 squares3 parts3 attnT0 mix1 add3
rootms3 top3 rms3 mix2 squares4 parts4 rootms4 attnT1 rope3 top4 rms4 mix3 proj0 attnT2 rope4 top5 mix4
attnT3 renewton0 cut7 rescale0 top6 proj1 mix5 attnT4 top7 attnT5 renewton1 mix6 rescale1 proj2 renorm0
attnT6 renewton2 rescale2 renorm1 mix7 proj3 attnT7 renorm2 renewton3 rescale3 proj4 renewton4 rescale4
up0 up1 hid0 renorm3 hid1 up2 up3 hid2 renorm4 hid3 up4 up5 hid4 hid5 up6 hid6 up7 up8 hid7 down0 hid8 up9
up10 hid9 hid10 up11 hid11 down1 down2 down3 down4""")
POOL_ORDER = _order("""
wp0 beta0 add1 cut0 cut1 cut2 add2 load0 load1 load2 cut3 cut4 add4 cut5 cut6""")
LOADS = [(0, 1), (1, 2), (2, 4), (4, KP)]
EARLY = 3


def build(nc, xT, wT, selT, tok_rows, wqkT, wvT, wpT, b_proj, gammas, betas, tab, tabT, maskT,
          wgT, wuT, wdT, out):
    f32, f32r = mybir.dt.float32, mybir.dt.float32r
    ALU, ACT, AX = mybir.AluOpType, mybir.ActivationFunctionType, mybir.AxisListType

    with ExitStack() as ctx:
        def sb(name, shape, dt=f32):
            return ctx.enter_context(nc.sbuf_tensor(name, shape, dt))

        def sem(name):
            return ctx.enter_context(nc.semaphore(name))

        x_in = sb("x_in", [P, KP, T])
        x_hi, x_lo = sb("x_hi", [P, KP, T], f32r), sb("x_lo", [P, KP, T], f32r)
        hid_hi, hid_lo = x_hi, x_lo
        w_in = sb("w_in", [P, KP, DIM])
        w_hi, w_lo = sb("w_hi", [P, KP, DIM], f32r), sb("w_lo", [P, KP, DIM], f32r)
        sel_in, sel = sb("sel_in", [TOK + 2, T]), sb("sel", [TOK + 2, T], f32r)
        rows_in = sb("rows_in", [TOK + 2, DIM])
        rows_hi, rows_lo = sb("rows_hi", [TOK + 2, DIM], f32r), sb("rows_lo", [TOK + 2, DIM], f32r)
        wqk_in = sb("wqk_in", [P, KD, 2 * DIM])
        wqk_mean = sb("wqk_mean", [P, KD, 2 * HEADS])
        wqk_hi, wqk_lo = sb("wqk_hi", [P, KD, 2 * DIM], f32r), sb("wqk_lo", [P, KD, 2 * DIM], f32r)
        wv_in = sb("wv_in", [P, KD, DIM])
        wv_hi, wv_lo = sb("wv_hi", [P, KD, DIM], f32r), sb("wv_lo", [P, KD, DIM], f32r)
        wp_in = sb("wp_in", [P, KD, DIM])
        wp_hi, wp_lo = sb("wp_hi", [P, KD, DIM], f32r), sb("wp_lo", [P, KD, DIM], f32r)
        bp_in = sb("bp_in", [1, DIM])
        bp_hi, bp_lo = sb("bp_hi", [1, DIM], f32r), sb("bp_lo", [1, DIM], f32r)
        one_row_in, one_row = sb("one_row_in", [1, P]), sb("one_row", [1, P], f32r)
        wg, wu = sb("wg", [P, KD, HIDDEN], f32r), sb("wu", [P, KD, HIDDEN], f32r)
        wd = sb("wd", [P, KH, DIM], f32r)
        gam = sb("gam", [P, 2, 2, HD])
        bet = sb("bet", [P, 2, 2])
        tab_sb = sb("tab_sb", [P, 2, NT, 2, HD])
        rope_a, rope_b = sb("rope_a", [P, NT, 2, HD]), sb("rope_b", [P, NT, 2, HD])
        tabT_sb = sb("tabT_sb", [P, 2, 2, TOK])
        bT = sb("bT", [P, 2, 2, TOK])
        betaT = sb("betaT", [P, 2, TOK])
        beta_all = sb("beta_all", [P, 2, IMAGES, TOK])
        mask = sb("mask", [P, CH])
        ident = sb("ident", [P, P])
        h0 = sb("h0", [P, NT, DIM])
        x1 = sb("x1", [P, NT, DIM])
        stats, mv = sb("stats", [P, 2, NT, 6]), sb("mv", [P, 2, NT, 2])
        log_var, guess, newton, rstd, shift = (
            sb(name, [P, 2 * NT]) for name in ("log_var", "guess", "newton", "rstd", "shift"))
        consts = sb("consts", [P, 4])
        lnT_hi, lnT_lo = sb("lnT_hi", [P, KD, T], f32r), sb("lnT_lo", [P, KD, T], f32r)
        square = sb("square", [P, 2, 2 * DIM])
        part_a, part_b = sb("part_a", [P, 2, 2 * DIM]), sb("part_b", [P, 2, 2 * DIM])
        qk = sb("qk", [P, 2, 2 * DIM])
        ssum, hlog, hguess = sb("ssum", [P, NT, 32]), sb("hlog", [P, NT, 32]), sb("hguess", [P, NT, 32])
        hnewton, hrstd = sb("hnewton", [P, NT, 32]), sb("hrstd", [P, NT, 32])
        qT, kT = sb("qT", [P, KD, T + 1]), sb("kT", [P, KD, T])
        k_heads = sb("k_heads", [P, K_RING, KD, CH, 2 * TOK])
        v_tok = sb("v_tok", [P, NT, REP, GROUPS, HV])
        v_rep = sb("v_rep", [P, V_RING, 2, REP, GROUPS, HV])
        top = sb("top", [P, 2, HEADS])
        x_room = x_in[:].rearrange("p k n -> p (k n)")
        w_room = [w[:].rearrange("p k n -> p (k n)") for w in (w_in, w_hi, w_lo)]
        logit = x_room[:, 0:T].rearrange("p (h k) -> p h k", k=TOK)
        prob = x_room[:, T:3 * T].rearrange("p (u n) -> p u n", u=2)
        probT = x_room[:, 3 * T:3 * T + 2 * GROUPS * ROWS].rearrange("p (u g n) -> p u g n", u=2, g=GROUPS)
        rsum = sb("rsum", [P, 2, HEADS])
        attn = sb("attn", [P, 2, HEADS, HD])
        attnT_hi, attnT_lo = (w[:, 0:KD * T].rearrange("p (c n) -> p c n", c=KD) for w in w_room[1:])
        ln = w_room[0][:, 0:NT * DIM].rearrange("p (t n) -> p t n", t=NT)
        silu = x_room[:, 0:T].rearrange("p (u n) -> p u n", u=2)
        hid = x_room[:, T:2 * T].rearrange("p (u n) -> p u n", u=2)
        res = h0

        ps = ctx.enter_context(nc.psum_tensor("ps", [P, 8, 512], f32))

        patch_in = [sem(f"patch_in{i}") for i in range(len(LOADS))]
        rows_loaded, wqk_loaded = sem("rows_loaded"), sem("wqk_loaded")
        wv_loaded, wp_loaded, tab_loaded = sem("wv_loaded"), sem("wp_loaded"), sem("tab_loaded")
        ffn_loaded = [sem(f"ffn_loaded{k}") for k in range(3)]
        ident_made, padded, ones_made = sem("ident_made"), sem("padded"), sem("ones_made")
        sel_hi_made, rows_lo_made = sem("sel_hi_made"), sem("rows_lo_made")
        patch_hi, patch_lo, w_lo_made = sem("patch_hi"), sem("patch_lo"), sem("w_lo_made")
        wqk_meaned, wqk_centred, wqk_hi_made, wqk_split = map(
            sem, ["wqk_meaned", "wqk_centred", "wqk_hi_made", "wqk_split"])
        wv_hi_made, wv_split, wp_split = sem("wv_hi_made"), sem("wv_split"), sem("wp_split")
        rope_made, tabs_step, beta_made = sem("rope_made"), sem("tabs_step"), sem("beta_made")
        embedded, h0_kept, stat_step, guess_step, newton_step, rstd_made, shift_made = map(
            sem, ["embedded", "h0_kept", "stat_step", "guess_step", "newton_step", "rstd_made", "shift_made"])
        normed, lnT_in, lnT_hi_made, lnT_split = map(
            sem, ["normed", "lnT_in", "lnT_hi_made", "lnT_split"])
        qk_in, squared, summed, hguess_step, hnewton_step, hrstd_made = map(
            sem, ["qk_in", "squared", "summed", "hguess_step", "hnewton_step", "hrstd_made"])
        consts_made = sem("consts_made")
        heads_cut = [sem(f"heads_cut{p}") for p in range(PAIRS)]
        parts_added = [sem(f"parts_added{t}") for t in range(NT)]
        parts_made, roped = sem("parts_made"), sem("roped")
        qkT_in, q_ready, k_ready = sem("qkT_in"), sem("q_ready"), sem("k_ready")
        v_in, v_kept = sem("v_in"), sem("v_kept")
        v_spread = [sem(f"v_spread{p}") for p in range(PAIRS)]
        scored, topped, shifted, prob_made = map(sem, ["scored", "topped", "shifted", "prob_made"])
        probT_in, probT_kept, mixed, rsum_made, attn_made = map(
            sem, ["probT_in", "probT_kept", "mixed", "rsum_made", "attn_made"])
        attnT_in, attnT_hi_made, attnT_split = map(sem, ["attnT_in", "attnT_hi_made", "attnT_split"])
        projected, x1_made = sem("projected"), sem("x1_made")
        gate_in, up_in, silu_made, hid_made, hid_hi_made, hid_split = map(
            sem, ["gate_in", "up_in", "silu_made", "hid_made", "hid_hi_made", "hid_split"])
        down_in = [sem(f"down_in{t}") for t in range(NT)]
        res_made, stored = sem("res_made"), sem("stored")

        SCORE_BANK, PT_BANK, MIX_BANK = 0, 2, 4
        LN_BANK, QK_BANK, VT_BANK = 5, 6, 7
        NORM_BANK = [LN_BANK, VT_BANK]
        GATE_BANK, UP_BANK = [2, 3], [0, 1]
        DOWN_BANK = [4, 5, 6, 7, 4]

        def ahead(stage, other):
            return sum(name == stage for name, _ in PE_ORDER[:PE_ORDER.index(other)])

        attnT_bank = ps[:, LN_BANK, 0:KD * P].rearrange("p (c j n) -> p c j n", c=KD, j=2)[:, :, :, 0:TOK]

        def attnT_of(attnT, p):
            return attnT[:, :, 2 * p * TOK:2 * (p + 1) * TOK].rearrange("p c (j n) -> p c j n", j=2)

        def load_of(k):
            return sum(k >= k1 for _, k1 in LOADS)

        def tile_for(tokens):
            return -(-tokens // P)

        def spreads(p):
            for b in (2 * p, 2 * p + 1):
                for t in range(b * TOK // P, tile_for((b + 1) * TOK)):
                    lo, hi = max(b * TOK, t * P), min((b + 1) * TOK, t * P + P)
                    for r in range(REP):
                        yield b, t, r, lo, hi

        def add_parts(queue, engine, t):
            n = TILES[t][1]
            queue.wait_ge(parts_made, 3 * (t + 1))
            engine.tensor_tensor(out=part_a[0:n, t % 2, :], in0=part_a[0:n, t % 2, :],
                                 in1=part_b[0:n, t % 2, :], op=ALU.add).then_inc(parts_added[t], 1)

        def cut_heads(queue, engine, p):
            queue.wait_ge(k_ready, tile_for(2 * (p + 1) * TOK))
            if p >= K_RING:
                queue.wait_ge(scored, p - K_RING + 1)
            engine.tensor_tensor(
                out=k_heads[:, p % K_RING],
                in0=kT[:, :, None, 2 * p * TOK:2 * (p + 1) * TOK].broadcast_to([P, KD, CH, 2 * TOK]),
                in1=mask[:, None, :, None].broadcast_to([P, KD, CH, 2 * TOK]),
                op=ALU.mult).then_inc(heads_cut[p], 1)

        block = ctx.enter_context(nc.Block())

        @block.sync
        def _(sp):
            for i, (k0, k1) in enumerate(LOADS):
                sp.dma_start(x_in[:, k0:k1, :], xT[:, k0:k1, :]).then_inc(patch_in[i], 16)
                if i == 0:
                    sp.dma_start(rows_in[:], tok_rows).then_inc(rows_loaded, 16)
                    sp.dma_start(sel_in[:], selT).then_inc(rows_loaded, 16)
            sp.dma_start(wqk_in[:], wqkT).then_inc(wqk_loaded, 16)
            sp.dma_start(tab_sb[:], tab).then_inc(tab_loaded, 16)
            sp.dma_start(gam[:], gammas).then_inc(tab_loaded, 16)
            sp.dma_start(bet[:], betas).then_inc(tab_loaded, 16)
            sp.dma_start(tabT_sb[:], tabT).then_inc(tab_loaded, 16)
            sp.dma_start(mask[:], maskT).then_inc(tab_loaded, 16)
            sp.dma_start(wv_in[:], wvT).then_inc(wv_loaded, 16)
            sp.dma_start(wp_in[:], wpT).then_inc(wp_loaded, 16)
            sp.dma_start(bp_in[:], b_proj).then_inc(wp_loaded, 16)
            sp.wait_ge(ones_made, 3)
            for p in range(PAIRS):
                sp.wait_ge(v_kept, 2 * tile_for(2 * (p + 1) * TOK))
                if p >= V_RING:
                    sp.wait_ge(mixed, p - V_RING + 1)
                for b, t, r, lo, hi in spreads(p):
                    k = r * TOK + lo - b * TOK
                    sp.dma_start(v_rep[k:k + hi - lo, p % V_RING, b % 2, r, :, :],
                                 v_tok[lo - t * P:hi - t * P, t, r, :, :]).then_inc(v_spread[p], 16)
            for t, (a, n) in enumerate(TILES):
                sp.wait_ge(res_made, t + 1)
                sp.dma_start(out[a:a + n, :], res[0:n, t, :]).then_inc(stored, 16)
            sp.wait_ge(stored, 16 * NT)

        @block.gpsimd
        def _(pool):
            nc.gpsimd.memset(ident[:], 0.0).then_inc(ident_made, 1)
            pool.wait_ge(ident_made, 1)
            nc.gpsimd.affine_select(out=ident[:], in_=ident[:], compare_op=ALU.not_equal, fill=1.0,
                                    base=0, pattern=[[-1, P]], channel_multiplier=1).then_inc(ident_made, 1)
            for i, c in enumerate((EPS, math.log(GUESS), EPS_HEAD, math.log(GUESS_HEAD))):
                nc.gpsimd.memset(consts[:, i:i + 1], c).then_inc(consts_made, 1)
            nc.gpsimd.memset(one_row_in[:], 1.0).then_inc(padded, 1)
            nc.gpsimd.memset(qT[:, :, T:T + 1], 0.0).then_inc(padded, 1)
            nc.gpsimd.memset(v_rep[:], 0.0).then_inc(ones_made, 1)
            nc.gpsimd.memset(v_tok[:, :, :, :, 0:HD], 0.0).then_inc(ones_made, 1)
            nc.gpsimd.memset(v_tok[:, :, :, :, HD:HV], 1.0).then_inc(ones_made, 1)
            for k in range(KP):
                pool.wait_ge(patch_hi, 2 * k + 2)
                nc.gpsimd.tensor_tensor(out=w_lo[:, k, :], in0=w_in[:, k, :],
                                        in1=w_hi[:, k, :].bitcast(f32), op=ALU.subtract
                                        ).then_inc(w_lo_made, 1)
            pool.wait_ge(wv_hi_made, 1)
            nc.gpsimd.tensor_tensor(out=wv_lo[:], in0=wv_in[:], in1=wv_hi[:].bitcast(f32),
                                    op=ALU.subtract).then_inc(wv_split, 1)
            pool.wait_ge(tab_loaded, 80)
            nc.gpsimd.tensor_tensor(out=rope_a[:], in0=tab_sb[:, 0],
                                    in1=gam[:, None, 0].broadcast_to([P, NT, 2, HD]),
                                    op=ALU.mult).then_inc(rope_made, 1)
            nc.gpsimd.tensor_tensor(out=rope_b[:], in0=tab_sb[:, 1],
                                    in1=gam[:, None, 1].broadcast_to([P, NT, 2, HD]),
                                    op=ALU.mult).then_inc(rope_made, 1)
            for j in range(2):
                for w in range(2):
                    nc.gpsimd.tensor_scalar(bT[:, j, w, :], tabT_sb[:, j, w, :], bet[:, j, w:w + 1],
                                            None, ALU.mult).then_inc(tabs_step, 1)
            pool.wait_ge(tabs_step, 4)
            nc.gpsimd.tensor_tensor(out=betaT[:], in0=bT[:, 0], in1=bT[:, 1],
                                    op=ALU.add).then_inc(tabs_step, 1)

            def spread_beta():
                pool.wait_ge(tabs_step, 5)
                nc.gpsimd.tensor_copy(beta_all[:], betaT[:, :, None, :].broadcast_to([P, 2, IMAGES, TOK])
                                      ).then_inc(beta_made, 1)

            def split(hi, lo, src, semaphore, n0):
                nc.gpsimd.tensor_copy(hi, src).then_inc(semaphore, 1)
                pool.wait_ge(semaphore, n0 + 1)
                nc.gpsimd.tensor_tensor(out=lo, in0=src, in1=hi.bitcast(f32),
                                        op=ALU.subtract).then_inc(semaphore, 1)

            def load_ffn(i):
                if i == 0:
                    for load in patch_in:
                        pool.wait_ge(load, 32)
                dst, src = [(wg, wgT), (wu, wuT), (wd, wdT)][i]
                pool.dma_start(dst[:], src).then_inc(ffn_loaded[i], 16)

            for kind, i in POOL_ORDER:
                if kind == "add":
                    add_parts(pool, nc.gpsimd, i)
                elif kind == "cut":
                    cut_heads(pool, nc.gpsimd, i)
                elif kind == "beta":
                    spread_beta()
                elif kind == "load":
                    load_ffn(i)
                else:
                    pool.wait_ge(wp_loaded, 32)
                    split(wp_hi[:], wp_lo[:], wp_in[:], wp_split, 0)
                    split(bp_hi[:], bp_lo[:], bp_in[:], wp_split, 2)

        @block.scalar
        def _(act):
            nc.scalar.preload_act_table_set("natural_log_exp_and_others")
            for i, (k0, k1) in enumerate(LOADS):
                act.dma_start(w_in[:, k0:k1, :], wT[:, k0:k1, :]).then_inc(patch_in[i], 16)
            for k in range(KP):
                act.wait_ge(patch_in[load_of(k)], 32)
                nc.scalar.copy(x_hi[:, k, :], x_in[:, k, :]).then_inc(patch_hi, 1)
                nc.scalar.copy(w_hi[:, k, :], w_in[:, k, :]).then_inc(patch_hi, 1)
                if k == 0:
                    act.wait_ge(rows_loaded, 32)
                    nc.scalar.copy(rows_hi[:], rows_in[:]).then_inc(sel_hi_made, 1)
                    nc.scalar.copy(sel[:], sel_in[:]).then_inc(sel_hi_made, 1)
            act.wait_ge(padded, 2)
            nc.scalar.copy(one_row[:], one_row_in[:]).then_inc(sel_hi_made, 1)
            act.wait_ge(wv_loaded, 16)
            nc.scalar.copy(wv_hi[:], wv_in[:]).then_inc(wv_hi_made, 1)

            def wqk_upper(_):
                act.wait_ge(wqk_centred, 1)
                nc.scalar.copy(wqk_hi[:], wqk_in[:]).then_inc(wqk_hi_made, 1)

            def guess_rstd(which, t):
                n, i = TILES[t][1], which * NT + t
                act.wait_ge(stat_step, 2 * i + 2)
                nc.scalar.activation(log_var[0:n, i:i + 1], mv[0:n, which, t, 1:2], ACT.Ln,
                                     bias=consts[0:n, 0:1]).then_inc(guess_step, 1)
                act.wait_ge(guess_step, 2 * i + 1)
                nc.scalar.activation(guess[0:n, i:i + 1], log_var[0:n, i:i + 1], ACT.Exp, scale=-0.5,
                                     bias=consts[0:n, 1:2]).then_inc(guess_step, 1)

            def apply_norm(which, t, src):
                n, i = TILES[t][1], which * NT + t
                act.wait_ge(shift_made, i + 1)
                if i == 0:
                    act.wait_ge(w_lo_made, KP)
                nc.scalar.activation(ln[0:n, t, :], src, ACT.Identity, bias=shift[0:n, i:i + 1],
                                     scale=rstd[0:n, i:i + 1]).then_inc(normed, 1)

            def keep_h0(t):
                n = TILES[t][1]
                act.wait_ge(stat_step, 2 * t + 1)
                nc.scalar.copy(h0[0:n, t, :], ps[0:n, t, 0:DIM]).then_inc(h0_kept, 1)

            def lnT_upper(which, t):
                a, n = TILES[t]
                act.wait_ge(lnT_in, which * NT + t + 1)
                nc.scalar.activation(lnT_hi[:, :, a:a + n],
                                     ps[:, NORM_BANK[which], 0:KD * n].rearrange("p (c n) -> p c n", c=KD),
                                     ACT.Copy, scale=-1.0).then_inc(lnT_hi_made, 1)

            def squares(t):
                n = TILES[t][1]
                act.wait_ge(qk_in, t + 1)
                if t >= 2:
                    act.wait_ge(summed, t - 1)
                nc.scalar.activation(square[0:n, t % 2, :], ps[0:n, QK_BANK, :], ACT.Square
                                     ).then_inc(squared, 1)

            def values(t):
                n = TILES[t][1]
                act.wait_ge(v_in, t + 1)
                if t == 0:
                    act.wait_ge(ones_made, 3)
                for r0, r1, g, c0, c1 in ((0, 2, 5, 0, 160), (2, 3, 6, 160, 256)):
                    nc.scalar.copy(v_tok[0:n, t, r0:r1, 0:g, 0:HD],
                                   ps[0:n, VT_BANK, c0:c1].rearrange("p (r g d) -> p r g d", g=g, d=HD)
                                   ).then_inc(v_kept, 1)

            def guess_heads(t):
                n = TILES[t][1]
                act.wait_ge(summed, t + 1)
                nc.scalar.activation(hlog[0:n, t, :], ssum[0:n, t, :], ACT.Ln, scale=1.0 / HD,
                                     bias=consts[0:n, 2:3]).then_inc(hguess_step, 1)
                act.wait_ge(hguess_step, 2 * t + 1)
                nc.scalar.activation(hguess[0:n, t, :], hlog[0:n, t, :], ACT.Exp, scale=-0.5,
                                     bias=consts[0:n, 3:4]).then_inc(hguess_step, 1)

            def exponentials(p):
                act.wait_ge(shifted, p + 1)
                if p >= 2:
                    act.wait_ge(probT_in, 2 * (p - 1))
                nc.scalar.activation(prob[0:ROWS, p % 2, :], logit[0:ROWS].rearrange("p h k -> p (h k)"),
                                     ACT.Exp).then_inc(prob_made, 1)

            def attnT_upper(p):
                act.wait_ge(attnT_in, p + 1)
                nc.scalar.copy(attnT_of(attnT_hi, p), attnT_bank).then_inc(attnT_hi_made, 1)

            def keep_probT(p):
                if p >= 2:
                    act.wait_ge(mixed, p - 1)
                for i in range(2):
                    act.wait_ge(probT_in, 2 * p + i + 1)
                    nc.scalar.copy(probT[0:REP * TOK, p % 2, 3 * i:3 * i + 3, :],
                                   ps[0:REP * TOK, PT_BANK + i, 0:3 * ROWS].rearrange("p (g n) -> p g n", g=3)
                                   ).then_inc(probT_kept, 1)

            def hidden_upper(u):
                half, j = divmod(u, KH)
                act.wait_ge(hid_made, u + 1)
                nc.scalar.copy(hid_hi[:, j, half * COLS:(half + 1) * COLS], hid[:, u % 2, :]
                               ).then_inc(hid_hi_made, 1)

            def gates(u):
                act.wait_ge(gate_in, u + 1)
                if u == 0:
                    act.wait_ge(prob_made, PAIRS)
                if u >= 2:
                    act.wait_ge(hid_made, u - 1)
                nc.scalar.activation(silu[:, u % 2, :], ps[:, GATE_BANK[u % 2], 0:COLS], ACT.Silu,
                                     scale=CODE_SCALE).then_inc(silu_made, 1)

            steps = {"embed": lambda t: guess_rstd(0, t), "wqk": wqk_upper,
                     "scale": lambda t: apply_norm(0, t, ps[0:TILES[t][1], t, 0:DIM]), "keep": keep_h0,
                     "norm": lambda t: lnT_upper(0, t), "qk": squares, "v": values, "rms": guess_heads,
                     "exp": exponentials, "probT": keep_probT, "attnT": attnT_upper,
                     "proj": lambda t: guess_rstd(1, t),
                     "rescale": lambda t: apply_norm(1, t, x1[0:TILES[t][1], t, :]),
                     "renorm": lambda t: lnT_upper(1, t), "gate": gates, "hid": hidden_upper}
            act.wait_ge(consts_made, 4)
            for stage, i in ACT_ORDER:
                steps[stage](i)

        @block.vector
        def _(dve):
            for k in range(KP):
                dve.wait_ge(patch_hi, 2 * k + 1)
                nc.vector.tensor_tensor(out=x_lo[:, k, :], in0=x_in[:, k, :],
                                        in1=x_hi[:, k, :].bitcast(f32), op=ALU.subtract
                                        ).then_inc(patch_lo, 1)
                if k == 0:
                    dve.wait_ge(sel_hi_made, 2)
                    nc.vector.tensor_tensor(out=rows_lo[:], in0=rows_in[:], in1=rows_hi[:].bitcast(f32),
                                            op=ALU.subtract).then_inc(rows_lo_made, 1)
            wqk_heads = wqk_in[:].rearrange("p c (h d) -> p (c h) d", d=HD)
            means = wqk_mean[:].rearrange("p c h -> p (c h)")

            def centre_wqk(_):
                dve.wait_ge(wqk_loaded, 16)
                nc.vector.tensor_reduce(means, wqk_heads, AX.X, ALU.add).then_inc(wqk_meaned, 1)
                dve.wait_ge(wqk_meaned, 1)
                nc.vector.scalar_tensor_tensor(out=wqk_heads, in0=means[:, :, None].broadcast_to([P, KD * 2 * HEADS, HD]),
                                               scalar=-1.0 / HD, in1=wqk_heads, op0=ALU.mult, op1=ALU.add
                                               ).then_inc(wqk_centred, 1)

            def wqk_lower(_):
                dve.wait_ge(wqk_hi_made, 1)
                nc.vector.tensor_tensor(out=wqk_lo[:], in0=wqk_in[:], in1=wqk_hi[:].bitcast(f32),
                                        op=ALU.subtract).then_inc(wqk_split, 1)

            def moments(which, t, src):
                n, i = TILES[t][1], which * NT + t
                nc.vector.bn_stats(stats[0:n, which, t, :], src).then_inc(stat_step, 1)
                dve.wait_ge(stat_step, 2 * i + 1)
                nc.vector.bn_aggr(mv[0:n, which, t, :], stats[0:n, which, t, :]).then_inc(stat_step, 1)

            def norm_scale(which, t):
                n, i = TILES[t][1], which * NT + t
                v, y, z = mv[0:n, which, t, 1:2], guess[0:n, i:i + 1], newton[0:n, i:i + 1]
                dve.wait_ge(guess_step, 2 * i + 2)
                nc.vector.tensor_tensor(out=z, in0=y, in1=y, op=ALU.mult).then_inc(newton_step, 1)
                dve.wait_ge(newton_step, 2 * i + 1)
                nc.vector.scalar_tensor_tensor(out=z, in0=v, scalar=EPS, in1=z, op0=ALU.add, op1=ALU.mult
                                               ).then_inc(newton_step, 1)

            def norm_shift(which, t):
                n, i = TILES[t][1], which * NT + t
                y, z, r = (a[0:n, i:i + 1] for a in (guess, newton, rstd))
                dve.wait_ge(newton_step, 2 * i + 2)
                nc.vector.scalar_tensor_tensor(out=r, in0=z, scalar=-3 * GUESS ** 2, in1=y,
                                               op0=ALU.add, op1=ALU.mult).then_inc(rstd_made, 1)
                dve.wait_ge(rstd_made, i + 1)
                nc.vector.scalar_tensor_tensor(out=shift[0:n, i:i + 1], in0=mv[0:n, which, t, 0:1],
                                               scalar=-1.0, in1=r, op0=ALU.mult,
                                               op1=ALU.mult).then_inc(shift_made, 1)

            def lnT_lower(which, t):
                a, n = TILES[t]
                dve.wait_ge(lnT_hi_made, which * NT + t + 1)
                nc.vector.scalar_tensor_tensor(
                    out=lnT_lo[:, :, a:a + n], in0=ps[:, NORM_BANK[which], 0:KD * n].rearrange("p (c n) -> p c n", c=KD),
                    scalar=-1.0, in1=lnT_hi[:, :, a:a + n].bitcast(f32), op0=ALU.mult, op1=ALU.subtract
                    ).then_inc(lnT_split, 1)

            def sum_squares(t):
                n = TILES[t][1]
                dve.wait_ge(squared, t + 1)
                nc.vector.tensor_reduce(ssum[0:n, t, :],
                                        square[0:n, t % 2, :].rearrange("p (h d) -> p h d", d=HD),
                                        AX.X, ALU.add).then_inc(summed, 1)

            def rope_parts(t):
                n = TILES[t][1]
                dve.wait_ge(squared, t + 1)
                if t == 0:
                    dve.wait_ge(rope_made, 2)
                if t >= 2:
                    dve.wait_ge(roped, t - 1)
                x = ps[0:n, QK_BANK, :].rearrange("p (w h d) -> p w h d", w=2, d=HD)
                a = part_a[0:n, t % 2, :].rearrange("p (w h d) -> p w h d", w=2, d=HD)
                b = part_b[0:n, t % 2, :].rearrange("p (w h d) -> p w h d", w=2, d=HD)
                nc.vector.tensor_tensor(out=a, in0=x,
                                        in1=rope_a[0:n, t, :, None].broadcast_to([n, 2, HEADS, HD]),
                                        op=ALU.mult).then_inc(parts_made, 1)
                for s in range(2):
                    o, i = slice(s * HALF, (s + 1) * HALF), slice((1 - s) * HALF, (2 - s) * HALF)
                    nc.vector.tensor_tensor(out=b[:, :, :, o], in0=x[:, :, :, i],
                                            in1=rope_b[0:n, t, :, None, o].broadcast_to([n, 2, HEADS, HALF]),
                                            op=ALU.mult).then_inc(parts_made, 1)

            def head_scale(t):
                n = TILES[t][1]
                v, y, z = (a[0:n, t, :] for a in (ssum, hguess, hnewton))
                dve.wait_ge(hguess_step, 2 * t + 2)
                nc.vector.tensor_tensor(out=z, in0=y, in1=y, op=ALU.mult).then_inc(hnewton_step, 1)
                dve.wait_ge(hnewton_step, 2 * t + 1)
                nc.vector.scalar_tensor_tensor(out=z, in0=v, scalar=HD * EPS_HEAD, in1=z, op0=ALU.add,
                                               op1=ALU.mult).then_inc(hnewton_step, 1)

            def scale_heads(t):
                n = TILES[t][1]
                y, z, r = (a[0:n, t, :] for a in (hguess, hnewton, hrstd))
                dve.wait_ge(hnewton_step, 2 * t + 2)
                nc.vector.scalar_tensor_tensor(out=r, in0=z, scalar=-3 * HD * GUESS_HEAD ** 2, in1=y,
                                               op0=ALU.add, op1=ALU.mult).then_inc(hrstd_made, 1)
                dve.wait_ge(hrstd_made, t + 1)
                dve.wait_ge(parts_added[t], 1)
                if t >= 2:
                    dve.wait_ge(qkT_in, t - 1)
                nc.vector.tensor_tensor(
                    out=qk[0:n, t % 2, :].rearrange("p (h d) -> p h d", d=HD),
                    in0=part_a[0:n, t % 2, :].rearrange("p (h d) -> p h d", d=HD),
                    in1=r[:, :, None].broadcast_to([n, 2 * HEADS, HD]),
                    op=ALU.mult).then_inc(roped, 1)

            def keep_qkT(t):
                a, n = TILES[t]
                dve.wait_ge(qkT_in, t + 1)
                if t == 0:
                    dve.wait_ge(beta_made, 1)
                src = ps[:, VT_BANK, 0:4 * n].rearrange("p (w c n) -> p w c n", w=2, c=KD)
                beta = beta_all[:].rearrange("p w b k -> p w (b k)")
                for w, (dst, ready) in enumerate(((qT, q_ready), (kT, k_ready))):
                    nc.vector.tensor_tensor(out=dst[:, :, a:a + n],
                                            in0=beta[:, w:w + 1, a:a + n].broadcast_to([P, KD, n]),
                                            in1=src[:, w], op=ALU.subtract).then_inc(ready, 1)

            def residual(t):
                n = TILES[t][1]
                dve.wait_ge(projected, t + 1)
                if t == 0:
                    dve.wait_ge(h0_kept, NT)
                nc.vector.tensor_tensor(out=x1[0:n, t, :], in0=ps[0:n, QK_BANK, 0:DIM], in1=h0[0:n, t, :],
                                        op=ALU.add).then_inc(x1_made, 1)
                dve.wait_ge(x1_made, t + 1)
                moments(1, t, x1[0:n, t, :])

            def take_top(p):
                dve.wait_ge(scored, p + 1)
                s = ps[0:ROWS, SCORE_BANK:SCORE_BANK + KD, 0:CH * TOK].rearrange("p c (h k) -> p c h k", k=TOK)
                tops = top[0:ROWS, p % 2, :].rearrange("p (c h) -> p c h", c=KD)
                nc.vector.tensor_reduce(tops, s, AX.X, ALU.max).then_inc(topped, 1)
                dve.wait_ge(topped, p + 1)
                if p >= 1:
                    dve.wait_ge(prob_made, p)
                nc.vector.tensor_tensor(out=logit[0:ROWS].rearrange("p (c h) k -> p c h k", c=KD), in0=s,
                                        in1=tops[:, :, :, None].broadcast_to([ROWS, KD, CH, TOK]),
                                        op=ALU.subtract).then_inc(shifted, 1)

            def normalise(p):
                dve.wait_ge(mixed, p + 1)
                o = ps[0:ROWS, MIX_BANK, 0:HEADS * HV].rearrange("p (h d) -> p h d", d=HV)
                nc.vector.reciprocal(rsum[0:ROWS, p % 2, :], o[:, :, HD]).then_inc(rsum_made, 1)
                dve.wait_ge(rsum_made, p + 1)
                if p >= 2:
                    dve.wait_ge(attnT_in, p - 1)
                nc.vector.tensor_tensor(out=attn[0:ROWS, p % 2], in0=o[:, :, 0:HD],
                                        in1=rsum[0:ROWS, p % 2, :, None].broadcast_to([ROWS, HEADS, HD]),
                                        op=ALU.mult).then_inc(attn_made, 1)

            def attnT_lower(p):
                dve.wait_ge(attnT_hi_made, p + 1)
                nc.vector.tensor_tensor(out=attnT_of(attnT_lo, p), in0=attnT_bank,
                                        in1=attnT_of(attnT_hi, p).bitcast(f32), op=ALU.subtract
                                        ).then_inc(attnT_split, 1)

            def hidden_lower(u):
                half, j = divmod(u, KH)
                cols = slice(half * COLS, (half + 1) * COLS)
                dve.wait_ge(hid_hi_made, u + 1)
                nc.vector.tensor_tensor(out=hid_lo[:, j, cols], in0=hid[:, u % 2, :],
                                        in1=hid_hi[:, j, cols].bitcast(f32), op=ALU.subtract
                                        ).then_inc(hid_split, 1)

            def result(t):
                n = TILES[t][1]
                dve.wait_ge(down_in[t], 1)
                nc.vector.scalar_tensor_tensor(out=res[0:n, t, :], in0=ps[0:n, DOWN_BANK[t], 0:DIM],
                                               scalar=CODE_SCALE, in1=x1[0:n, t, :],
                                               op0=ALU.mult, op1=ALU.add).then_inc(res_made, 1)

            def hidden(u):
                dve.wait_ge(silu_made, u + 1)
                dve.wait_ge(up_in, u + 1)
                if u == 0:
                    dve.wait_ge(probT_in, 2 * (PAIRS - 1))
                if u >= 2:
                    dve.wait_ge(hid_split, u - 1)
                nc.vector.scalar_tensor_tensor(out=hid[:, u % 2, :], in0=ps[:, UP_BANK[u % 2], 0:COLS],
                                               scalar=CODE_SCALE, in1=silu[:, u % 2, :],
                                               op0=ALU.mult, op1=ALU.mult).then_inc(hid_made, 1)

            def first_moments(t):
                dve.wait_ge(embedded, t + 1)
                moments(0, t, ps[0:TILES[t][1], t, 0:DIM])

            steps = {"embed": first_moments, "centre": centre_wqk, "wqk": wqk_lower,
                     "newton": lambda t: norm_scale(0, t), "scale": lambda t: norm_shift(0, t),
                     "norm": lambda t: lnT_lower(0, t),
                     "squares": sum_squares, "parts": rope_parts,
                     "add": lambda t: add_parts(dve, nc.vector, t),
                     "cut": lambda p: cut_heads(dve, nc.vector, p), "rootms": head_scale, "rms": scale_heads, "rope": keep_qkT,
                     "top": take_top, "mix": normalise, "attnT": attnT_lower, "proj": residual,
                     "renewton": lambda t: norm_scale(1, t), "rescale": lambda t: norm_shift(1, t), "renorm": lambda t: lnT_lower(1, t),
                     "up": hidden, "hid": hidden_lower, "down": result}
            dve.wait_ge(tab_loaded, 80)
            for stage, i in DVE_ORDER:
                steps[stage](i)

        @block.tensor
        def _(pe):
            def split_product(dst, steps, first=True, last=True):
                for i, (lhs, rhs) in enumerate(steps):
                    m = nc.tensor.matmul(dst, lhs, rhs, start=first and i == 0,
                                         stop=last and i == len(steps) - 1)
                return m

            def embed(t, k):
                a, n = TILES[t]
                pe.wait_ge(patch_hi, 2 * k + 2)
                pe.wait_ge(patch_lo, k + 1)
                pe.wait_ge(w_lo_made, k + 1)
                split_product(ps[0:n, t, 0:DIM],
                              [(x_hi[:, k, a:a + n], w_hi[:, k, :]), (x_hi[:, k, a:a + n], w_lo[:, k, :]),
                               (x_lo[:, k, a:a + n], w_hi[:, k, :])], k == 0, False)

            def finish_embedding(t):
                a, n = TILES[t]
                for k in range(EARLY, KP):
                    embed(t, k)
                pe.wait_ge(rows_lo_made, 1)
                split_product(ps[0:n, t, 0:DIM], [(sel[:, a:a + n], rows_hi[:]), (sel[:, a:a + n], rows_lo[:])],
                              False, True).then_inc(embedded, 1)

            for k in range(EARLY):
                for t in range(NT):
                    embed(t, k)

            def transpose_ln(which, t):
                n, i = TILES[t][1], which * NT + t
                pe.wait_ge(normed, i + 1)
                if i == 0:
                    pe.wait_ge(ident_made, 2)
                if i == NT:
                    pe.wait_ge(v_kept, 2 * NT)
                    pe.wait_ge(k_ready, NT)
                elif i >= 1:
                    pe.wait_ge(lnT_split, i)
                for c in range(KD):
                    m = nc.tensor.transpose(ps[:, NORM_BANK[which], c * n:(c + 1) * n],
                                            ln[0:n, t, c * P:(c + 1) * P], ident[0:n, 0:n])
                m.then_inc(lnT_in, 1)

            both = [(w, c) for w in range(3) for c in range(KD)]
            lhs = [lnT_hi, lnT_hi, lnT_lo]

            def project_qk(t):
                a, n = TILES[t]
                pe.wait_ge(lnT_split, t + 1)
                if t == 0:
                    pe.wait_ge(wqk_split, 1)
                else:
                    pe.wait_ge(parts_made, 3 * t)
                split_product(ps[0:n, QK_BANK, :],
                              [(lhs[w][:, c, a:a + n], [wqk_hi, wqk_lo, wqk_hi][w][:, c, :]) for w, c in both]
                              ).then_inc(qk_in, 1)

            def project_v(t):
                a, n = TILES[t]
                pe.wait_ge(lnT_split, t + 1)
                if t == 0:
                    pe.wait_ge(wv_split, 1)
                else:
                    pe.wait_ge(v_kept, 2 * t)
                if ahead("rope", ("v", t)):
                    pe.wait_ge(k_ready, ahead("rope", ("v", t)))
                split_product(ps[0:n, VT_BANK, 0:DIM],
                              [(lhs[w][:, c, a:a + n], [wv_hi, wv_lo, wv_hi][w][:, c, :]) for w, c in both]
                              ).then_inc(v_in, 1)

            def transpose_qk(t):
                n = TILES[t][1]
                pe.wait_ge(roped, t + 1)
                pe.wait_ge(v_kept, 2 * ahead("v", ("rope", t)))
                if t >= 1:
                    pe.wait_ge(k_ready, t)
                for w in range(4):
                    m = nc.tensor.transpose(ps[:, VT_BANK, w * n:(w + 1) * n],
                                            qk[0:n, t % 2, w * P:(w + 1) * P], ident[0:n, 0:n])
                m.then_inc(qkT_in, 1)

            def project_out(t):
                a, n = TILES[t]
                pe.wait_ge(attnT_split, min(PAIRS, -(-(a + n) // (2 * TOK))))
                if t == 0:
                    pe.wait_ge(wp_split, 4)
                    pe.wait_ge(sel_hi_made, 3)
                    pe.wait_ge(parts_made, 3 * NT)
                else:
                    pe.wait_ge(x1_made, t)
                steps = [(one_row[:, 0:n], bp_hi[:]), (one_row[:, 0:n], bp_lo[:])]
                for c in range(KD):
                    steps += [(attnT_hi[:, c, a:a + n], wp_hi[:, c, :]), (attnT_hi[:, c, a:a + n], wp_lo[:, c, :]),
                              (attnT_lo[:, c, a:a + n], wp_hi[:, c, :])]
                split_product(ps[0:n, QK_BANK, 0:DIM], steps).then_inc(projected, 1)

            def score(p):
                pe.wait_ge(heads_cut[p], 1)
                pe.wait_ge(q_ready, tile_for(min(T, (2 * p + 1) * TOK + WIDE[1])))
                if p == 0:
                    pe.wait_ge(padded, 2)
                    pe.wait_ge(h0_kept, SCORE_BANK + 2)
                else:
                    pe.wait_ge(shifted, p)
                for j in range(2):
                    a = (2 * p + j) * TOK
                    for c in range(KD):
                        m = nc.tensor.matmul(ps[64 * j:64 * j + WIDE[j], SCORE_BANK + c, 0:CH * TOK],
                                             qT[:, c, a:a + WIDE[j]],
                                             k_heads[:, p % K_RING, c, :, j * TOK:(j + 1) * TOK],
                                             start=True, stop=True)
                m.then_inc(scored, 1)

            def transpose_prob(p):
                pe.wait_ge(prob_made, p + 1)
                if p == 0:
                    pe.wait_ge(h0_kept, PT_BANK + 2)
                for g in range(GROUPS):
                    if p >= 1 and g % 3 == 0:
                        pe.wait_ge(probT_kept, 2 * (p - 1) + g // 3 + 1)
                    a = GROUP_HEAD[g] * TOK
                    m = nc.tensor.transpose(ps[0:REP * TOK, PT_BANK + g // 3, (g % 3) * ROWS:(g % 3 + 1) * ROWS],
                                            prob[0:ROWS, p % 2, a:a + REP * TOK], ident[0:ROWS, 0:ROWS])
                    if g % 3 == 2:
                        m.then_inc(probT_in, 1)

            def mix(p):
                pe.wait_ge(probT_kept, 2 * (p + 1))
                pe.wait_ge(v_spread[p], 16 * len(list(spreads(p))))
                if p == 0:
                    pe.wait_ge(h0_kept, MIX_BANK + 1)
                else:
                    pe.wait_ge(attn_made, p)
                for j in range(2):
                    q = slice(64 * j, 64 * j + WIDE[j])
                    for g in range(GROUPS):
                        if g < GROUPS - 1:
                            cols = slice(g * REP * HV, (g + 1) * REP * HV)
                            v = v_rep[0:REP * TOK, p % V_RING, j, :, g, :]
                        else:
                            cols = slice(15 * HV, 16 * HV)
                            v = v_rep[0:REP * TOK, p % V_RING, j, REP - 1, g, :]
                        m = nc.tensor.matmul(ps[q, MIX_BANK, cols], probT[0:REP * TOK, p % 2, g, q], v,
                                             start=True, stop=True)
                m.then_inc(mixed, 1)

            def transpose_attn(p):
                pe.wait_ge(attn_made, p + 1)
                if p == 0:
                    pe.wait_ge(lnT_split, NT)
                else:
                    pe.wait_ge(attnT_split, p)
                flat = attn[0:ROWS, p % 2].rearrange("p h d -> p (h d)")
                for c in range(KD):
                    m = nc.tensor.transpose(ps[:, LN_BANK, c * P:c * P + ROWS],
                                            flat[:, c * P:(c + 1) * P], ident[0:ROWS, 0:ROWS])
                m.then_inc(attnT_in, 1)

            def gate_up(u):
                half, j = divmod(u, KH)
                pe.wait_ge(lnT_split, NT + tile_for((half + 1) * COLS))
                cols, units = slice(half * COLS, (half + 1) * COLS), slice(j * P, (j + 1) * P)
                if u == 0:
                    pe.wait_ge(ffn_loaded[0], 16)
                    pe.wait_ge(ffn_loaded[1], 16)
                    pe.wait_ge(probT_kept, 2 * PAIRS)
                    pe.wait_ge(shifted, PAIRS)
                if u >= 2:
                    pe.wait_ge(silu_made, u - 1)
                split_product(ps[:, GATE_BANK[u % 2], 0:COLS],
                              [(wg[:, c, units], x[:, c, cols]) for c in range(KD) for x in (lnT_hi, lnT_lo)]
                              ).then_inc(gate_in, 1)
                if u >= 2:
                    pe.wait_ge(hid_made, u - 1)
                split_product(ps[:, UP_BANK[u % 2], 0:COLS],
                              [(wu[:, c, units], x[:, c, cols]) for c in range(KD) for x in (lnT_hi, lnT_lo)]
                              ).then_inc(up_in, 1)

            def down_product(t, units, last):
                a, n = TILES[t]
                return split_product(ps[0:n, DOWN_BANK[t], 0:DIM],
                                     [(h[:, j, a:a + n], wd[:, j, :]) for j in units for h in (hid_hi, hid_lo)],
                                     units[0] == 0, last)

            def down(t):
                pe.wait_ge(hid_split, KH)
                if t == 0:
                    pe.wait_ge(ffn_loaded[2], 16)
                    pe.wait_ge(attn_made, PAIRS)
                    pe.wait_ge(attnT_split, PAIRS)
                down_product(t, range(KH), True).then_inc(down_in[t], 1)

            def down_step(j):
                pe.wait_ge(hid_split, KH + j + 1)
                if j == 0:
                    pe.wait_ge(x1_made, NT)
                    pe.wait_ge(lnT_split, 2 * NT)
                    pe.wait_ge(res_made, 1)
                for t in range(2, NT):
                    m = down_product(t, [j], j == KH - 1)
                    if j == KH - 1:
                        m.then_inc(down_in[t], 1)

            steps = {"embed": finish_embedding, "norm": lambda t: transpose_ln(0, t), "qk": project_qk,
                     "v": project_v, "rope": transpose_qk, "score": score, "probT": transpose_prob,
                     "mix": mix, "attnT": transpose_attn, "proj": project_out,
                     "renorm": lambda t: transpose_ln(1, t), "ffn": gate_up, "down": down,
                     "step": down_step}
            for stage, i in PE_ORDER:
                steps[stage](i)


def _chunks(a):
    k = a.shape[0] // P
    return np.ascontiguousarray(a.reshape(k, P, -1).transpose(1, 0, 2))


def _rotary():
    inv = (1.0 / np.float32(10000.0) ** (np.arange(HALF, dtype=np.float32) / np.float32(HALF))).astype(np.float32)
    freq = np.outer(np.arange(TOK, dtype=np.float32), inv).astype(np.float32)
    cos = np.cos(np.concatenate([freq, freq], -1))
    sin = np.sin(np.concatenate([-freq, freq], -1))
    scale = np.float32(HD ** -0.5)
    return np.stack([np.stack([cos * scale, cos]), np.stack([sin * scale, sin])]).astype(np.float32)


def kernel(x, L0_tok_W, L0_tok_b, L0_tok_cls_token, L0_tok_pos_embed, L0_attn_w_qkv, L0_attn_w_proj,
           L0_attn_b_proj, L0_attn_q_gamma, L0_attn_q_beta, L0_attn_k_gamma, L0_attn_k_beta,
           L0_ffn_w_gate, L0_ffn_w_up, L0_ffn_w_down):
    import concourse.bacc as bacc
    from concourse.bass_utils import run_bass_kernel_spmd

    x = np.asarray(x)
    f = np.float32
    patches = x.reshape(IMAGES, CHANNELS, GRID, PATCH, GRID, PATCH).transpose(1, 3, 5, 0, 2, 4)
    cols = np.zeros((PATCH_DIM, IMAGES, TOK), f)
    cols[:, :, 1:] = patches.reshape(PATCH_DIM, IMAGES, TOK - 1)
    sel = np.zeros((TOK + 2, IMAGES, TOK), f)
    for k in range(TOK):
        sel[k, :, k] = 1
    sel[TOK, :, 1:] = 1
    sel[TOK + 1, :, 0] = 1
    tok_rows = np.concatenate([np.asarray(L0_tok_pos_embed).reshape(TOK, DIM), np.asarray(L0_tok_b).reshape(1, DIM),
                               np.asarray(L0_tok_cls_token).reshape(1, DIM)])
    w_qkv, w_proj = np.asarray(L0_attn_w_qkv), np.asarray(L0_attn_w_proj)
    heads = np.arange(DIM).reshape(HEADS, HD)
    v_rows = np.concatenate([heads[h] for group in VALUE_HEADS for h in group])
    rot = _rotary()
    pos = np.arange(NT * P) % TOK
    tab = rot[:, :, pos, :].reshape(2, 2, NT, P, HD).transpose(3, 0, 2, 1, 4)
    tabT = np.tile(rot.transpose(3, 0, 1, 2), (P // HD, 1, 1, 1))
    swap = np.r_[HALF:HD, 0:HALF]
    g = [np.asarray(L0_attn_q_gamma), np.asarray(L0_attn_k_gamma)]
    b = [np.asarray(L0_attn_q_beta), np.asarray(L0_attn_k_beta)]
    gammas = np.broadcast_to(np.stack([np.stack(g), np.stack([v[swap] for v in g])]), (P, 2, 2, HD))
    betas = np.tile(np.stack([np.stack(b, -1), np.stack([v[swap] for v in b], -1)], 1), (P // HD, 1, 1))

    arrays = {
        "xT": _chunks(cols.reshape(PATCH_DIM, T)),
        "wT": _chunks(np.asarray(L0_tok_W).T),
        "selT": sel.reshape(TOK + 2, T),
        "tok_rows": tok_rows,
        "wqkT": _chunks(w_qkv[:2 * DIM].T),
        "wvT": _chunks(w_qkv[2 * DIM:][v_rows].T),
        "wpT": _chunks(w_proj.T),
        "b_proj": np.asarray(L0_attn_b_proj).reshape(1, DIM),
        "gammas": gammas,
        "betas": betas,
        "tab": tab,
        "tabT": tabT,
        "maskT": np.repeat(np.eye(CH, dtype=f), HD, axis=0),
        "wgT": _chunks(np.asarray(L0_ffn_w_gate).T),
        "wuT": _chunks(np.asarray(L0_ffn_w_up).T),
        "wdT": _chunks(np.asarray(L0_ffn_w_down).T),
    }
    nc = bacc.Bacc("TRN2", target_bir_lowering=False, num_devices=1)
    given, args = {}, {}
    for name, a in arrays.items():
        a = np.ascontiguousarray(a)
        given[f"in_{name}"] = a
        args[name] = nc.dram_tensor(f"in_{name}", a.shape, mybir.dt.from_np(a.dtype), kind="ExternalInput").ap()
    out = nc.dram_tensor("out", (T, DIM), mybir.dt.float32, kind="ExternalOutput").ap()
    build(nc, out=out, **args)
    r = run_bass_kernel_spmd(nc, [given], core_ids=[0])
    return r.results[0]["out"].reshape(IMAGES, TOK, DIM)
```
